# Optimizing a Trainium2 kernel written in Bass

```python
import numpy as np
import jax
import jax.numpy as jnp

def _softmax(x, axis=-1):
    return jax.nn.softmax(x, axis=axis)

def _gelu(x):
    return jax.nn.gelu(x, approximate=True)

def _silu(x):
    return jax.nn.silu(x)

def _sigmoid(x):
    return jax.nn.sigmoid(x)

def _layernorm(x, axis=-1, eps=1e-05):
    m = jnp.mean(x, axis=axis, keepdims=True)
    v = jnp.var(x, axis=axis, keepdims=True)
    return (x - m) / jnp.sqrt(v + eps)

def _scatter_add(tgt, idx, src, axis=0):
    return tgt.at[idx].add(src)

def _segment_sum(src, seg, n):
    return jax.ops.segment_sum(src, seg, n)
kernel_name = 'mk_audio_tower_d1_tok_audfeat512_r4_f529a3'

def setup_inputs(seed: int=0):
    np.random.seed(seed)
    _w = jnp.asarray

    def _rec_inputs():
        import jax
        import jax.numpy as jnp
        _rk = jax.random.key(seed)
        x = -3.53888e-05 + 1.00021 * jax.random.normal(jax.random.fold_in(_rk, 1), (8, 750, 23), jnp.float32)
        return x
    x = _rec_inputs()

    def _L0_tok_setup():
        import jax, jax.numpy as jnp
        import numpy as np
        CONTEXT = 5
        DILATION = 1
        BN_EPS = 1e-05

        def _tdnn_forward(x, W, b, gamma, beta):
            B, T, D = x.shape
            L = T - (CONTEXT - 1) * DILATION
            frames = jnp.stack([jax.lax.dynamic_slice_in_dim(x, k * DILATION, L, axis=1) for k in range(CONTEXT)], axis=2)
            patches = frames.reshape(B, L, CONTEXT * D)
            y = jnp.einsum('blf,of->blo', patches, W) + b
            y = jax.nn.relu(y)
            mean = jnp.mean(y, axis=(0, 1))
            var = jnp.var(y, axis=(0, 1))
            y = (y - mean) * jax.lax.rsqrt(var + BN_EPS) * gamma + beta
            return y
        key = jax.random.key(seed)
        k1, k2, k3 = jax.random.split(key, 3)
        B, T, D, O = (64, 1024, 23, 128)
        x = jax.random.normal(k1, (B, T, D), dtype=jnp.float32)
        fan_in = D * CONTEXT
        bound = 1.0 / np.sqrt(fan_in)
        W = jax.random.uniform(k2, (O, fan_in), dtype=jnp.float32, minval=-bound, maxval=bound)
        b = jax.random.uniform(k3, (O,), dtype=jnp.float32, minval=-bound, maxval=bound)
        gamma = jnp.ones((O,), dtype=jnp.float32)
        beta = jnp.zeros((O,), dtype=jnp.float32)
        return {'x': x, 'W': W, 'b': b, 'gamma': gamma, 'beta': beta}
    _L0_tok_all = _L0_tok_setup()
    _L0_tok_in = {k: v for k, v in _L0_tok_all.items() if k in ('W', 'b', 'gamma', 'beta')}
    del _L0_tok_all

    def _L0_attn_setup():
        import jax, jax.numpy as jnp
        import numpy as np
        B, T, I, H, O = (32, 128, 128, 256, 128)
        key = jax.random.key(seed)
        ks = jax.random.split(key, 7)
        s_ih = 1.0 / np.sqrt(H)
        s_lin = 1.0 / np.sqrt(H)
        return {'x': jax.random.normal(ks[0], (B, T, I), dtype=jnp.float32), 'W_ih': jax.random.uniform(ks[1], (H, I), jnp.float32, -s_ih, s_ih), 'W_hh': jax.random.uniform(ks[2], (H, H), jnp.float32, -s_ih, s_ih), 'b_ih': jax.random.uniform(ks[3], (H,), jnp.float32, -s_ih, s_ih), 'b_hh': jax.random.uniform(ks[4], (H,), jnp.float32, -s_ih, s_ih), 'W_out': jax.random.uniform(ks[5], (O, H), jnp.float32, -s_lin, s_lin), 'b_out': jax.random.uniform(ks[6], (O,), jnp.float32, -s_lin, s_lin)}
    _L0_attn_all = _L0_attn_setup()
    _L0_attn_in = {k: v for k, v in _L0_attn_all.items() if k in ('W_ih', 'W_hh', 'b_ih', 'b_hh', 'W_out', 'b_out')}
    del _L0_attn_all

    def _L0_ffn_setup():
        import jax, jax.numpy as jnp
        import numpy as np
        B, T, H = (8, 2048, 128)
        E, R = (4, 16)
        SCALE = 0.04
        key = jax.random.key(seed)
        ks = jax.random.split(key, 7)
        return {'x': jax.random.normal(ks[0], (B, T, H), jnp.float32), 'gate_w': jax.random.normal(ks[1], (E, H), jnp.float32) * SCALE, 'thr_w': jax.random.normal(ks[2], (1, H), jnp.float32) * SCALE, 'fc1_w': jax.random.normal(ks[3], (E, H, H), jnp.float32) * SCALE, 'lora_A': jax.random.normal(ks[4], (E, H, R), jnp.float32) * SCALE, 'lora_B': jax.random.normal(ks[5], (E, R, H), jnp.float32) * SCALE, 'fc2_w': jax.random.normal(ks[6], (E, H, H), jnp.float32) * SCALE}
    _L0_ffn_all = _L0_ffn_setup()
    _L0_ffn_in = {k: v for k, v in _L0_ffn_all.items() if k in ('gate_w', 'thr_w', 'fc1_w', 'lora_A', 'lora_B', 'fc2_w')}
    del _L0_ffn_all
    return {'x': x, 'L0_tok_W': _L0_tok_in['W'], 'L0_tok_b': _L0_tok_in['b'], 'L0_tok_gamma': _L0_tok_in['gamma'], 'L0_tok_beta': _L0_tok_in['beta'], 'L0_attn_W_ih': _L0_attn_in['W_ih'], 'L0_attn_W_hh': _L0_attn_in['W_hh'], 'L0_attn_b_ih': _L0_attn_in['b_ih'], 'L0_attn_b_hh': _L0_attn_in['b_hh'], 'L0_attn_W_out': _L0_attn_in['W_out'], 'L0_attn_b_out': _L0_attn_in['b_out'], 'L0_ffn_gate_w': _L0_ffn_in['gate_w'], 'L0_ffn_thr_w': _L0_ffn_in['thr_w'], 'L0_ffn_fc1_w': _L0_ffn_in['fc1_w'], 'L0_ffn_lora_A': _L0_ffn_in['lora_A'], 'L0_ffn_lora_B': _L0_ffn_in['lora_B'], 'L0_ffn_fc2_w': _L0_ffn_in['fc2_w']}

def reference(x, L0_tok_W, L0_tok_b, L0_tok_gamma, L0_tok_beta, L0_attn_W_ih, L0_attn_W_hh, L0_attn_b_ih, L0_attn_b_hh, L0_attn_W_out, L0_attn_b_out, L0_ffn_gate_w, L0_ffn_thr_w, L0_ffn_fc1_w, L0_ffn_lora_A, L0_ffn_lora_B, L0_ffn_fc2_w):
    import jax
    import jax.numpy as jnp

    def _L0_tok_ref(x, W, b, gamma, beta):
        import jax, jax.numpy as jnp
        import numpy as np
        CONTEXT = 5
        DILATION = 1
        BN_EPS = 1e-05

        def _tdnn_forward(x, W, b, gamma, beta):
            B, T, D = x.shape
            L = T - (CONTEXT - 1) * DILATION
            frames = jnp.stack([jax.lax.dynamic_slice_in_dim(x, k * DILATION, L, axis=1) for k in range(CONTEXT)], axis=2)
            patches = frames.reshape(B, L, CONTEXT * D)
            y = jnp.einsum('blf,of->blo', patches, W) + b
            y = jax.nn.relu(y)
            mean = jnp.mean(y, axis=(0, 1))
            var = jnp.var(y, axis=(0, 1))
            y = (y - mean) * jax.lax.rsqrt(var + BN_EPS) * gamma + beta
            return y
        return _tdnn_forward(x, W, b, gamma, beta)

    def _L0_attn_ref(x, W_ih, W_hh, b_ih, b_hh, W_out, b_out):
        import jax, jax.numpy as jnp
        import numpy as np
        B, T, I, H, O = (32, 128, 128, 256, 128)
        xp = jnp.einsum('bti,hi->bth', x, W_ih) + b_ih + b_hh
        h0 = jnp.zeros((x.shape[0], W_hh.shape[0]), dtype=x.dtype)

        def step(h, xp_t):
            h = jax.nn.relu(xp_t + h @ W_hh.T)
            return (h, h)
        _, hs = jax.lax.scan(step, h0, jnp.swapaxes(xp, 0, 1))
        hs = jnp.swapaxes(hs, 0, 1)
        return jnp.einsum('bth,oh->bto', hs, W_out) + b_out

    def _L0_ffn_ref(x, gate_w, thr_w, fc1_w, lora_A, lora_B, fc2_w):
        import jax, jax.numpy as jnp
        import numpy as np
        B, T, H = (8, 2048, 128)
        E, R = (4, 16)
        SCALE = 0.04
        b, t, h = x.shape
        e = gate_w.shape[0]
        xf = x.reshape(-1, h)
        gate_logits = jax.nn.softmax(xf @ gate_w.T, axis=-1)
        thresholds = jax.nn.sigmoid(xf @ thr_w.T) * (1.0 / e)
        adapted = gate_logits - thresholds
        selected = (adapted >= 0).astype(xf.dtype)
        weights = adapted * selected
        wsum = jnp.sum(weights, axis=-1, keepdims=True)
        wsum = jnp.where(wsum == 0, jnp.ones_like(wsum), wsum)
        weights = weights / wsum
        hidden = jax.nn.relu(jnp.einsum('ni,ehi->neh', xf, fc1_w))
        lo = jnp.einsum('neh,ehr->ner', hidden, lora_A)
        lo = jnp.einsum('ner,ero->neo', lo, lora_B)
        expert_out = jnp.einsum('neo,edo->ned', lo, fc2_w)
        out = jnp.einsum('ne,ned->nd', weights, expert_out)
        return out.reshape(b, t, h)
    h = _L0_tok_ref(x, L0_tok_W, L0_tok_b, L0_tok_gamma, L0_tok_beta)
    h = h + _L0_attn_ref(_layernorm(h, axis=-1), L0_attn_W_ih, L0_attn_W_hh, L0_attn_b_ih, L0_attn_b_hh, L0_attn_W_out, L0_attn_b_out)
    h = h + _L0_ffn_ref(_layernorm(h, axis=-1), L0_ffn_gate_w, L0_ffn_thr_w, L0_ffn_fc1_w, L0_ffn_lora_A, L0_ffn_lora_B, L0_ffn_fc2_w)
    return h

_drawn_inputs = setup_inputs


def setup_inputs(seed=0):
    import zlib

    import numpy as np

    out = dict(_drawn_inputs(seed))
    spreads = {'L0_tok_gamma': (1.0, 0.2), 'L0_tok_beta': (0.0, 0.1)}
    factors = {'L0_attn_b_ih': 4.233,
     'L0_attn_b_hh': 3.959,
     'L0_ffn_gate_w': 8.0,
     'L0_ffn_thr_w': 8.0,
     'L0_ffn_fc1_w': 8.0,
     'L0_ffn_lora_A': 8.0,
     'L0_ffn_lora_B': 8.0,
     'L0_ffn_fc2_w': 8.0}
    for name, (base, spread) in spreads.items():
        noise = np.random.default_rng([zlib.crc32(name.encode()), seed]).standard_normal(out[name].shape)
        drawn = base * np.exp(spread * noise) if base else spread * noise
        out[name] = jnp.asarray(drawn.astype(out[name].dtype))
    for name, factor in factors.items():
        out[name] = (out[name] * factor).astype(out[name].dtype)
    return out
```

```python
from contextlib import ExitStack

import concourse.bass as bass
from concourse import mybir

ALU = mybir.AluOpType
ACT = mybir.ActivationFunctionType
AX_X = mybir.AxisListType.X
F32 = mybir.dt.float32
I32 = mybir.dt.int32

P = 128
EPS = 1e-5


def audio_tower(nc, x, tok_w, tok_b, tok_gamma, tok_beta, w_ih, w_hh, b_ih, b_hh, w_out, b_out,
                gate_w, thr_w, fc1_w, lora_a, lora_b, fc2_w, out):
    B, T, D = x.shape
    FEAT, PATCH = tok_w.shape
    CONTEXT = PATCH // D
    HID = w_hh.shape[0]
    KH = HID // P
    E, R = lora_a.shape[0], lora_a.shape[2]
    L = T - CONTEXT + 1
    CHUNKS = P // B
    G = 4
    STEPS = -(-L // (CHUNKS * G)) * G
    GROUPS = STEPS // G
    WARM = 20
    LAST = L - (CHUNKS - 1) * STEPS
    W = G * P
    XW = (G + CONTEXT - 1) * D
    ER = 32
    FULL = LAST // G
    CUT = LAST % G
    TOL = 2.0 ** -20
    assert KH == 2 and FEAT == P and E * ER == P and GROUPS % 2 == 0 and WARM % G == 0
    assert FULL % 2 == 0 and 0 < CUT < G and LAST > 0 and WARM // G == GROUPS // 2 - 1
    COLS = (CHUNKS - 1) * B

    with ExitStack() as ctx:
        def sb(name, shape, dt=F32):
            return ctx.enter_context(nc.sbuf_tensor(name, shape, dt))

        def sem(name):
            return ctx.enter_context(nc.semaphore(name))

        ident = sb("ident", [P, P])
        tokw_raw = sb("tokw_raw", [P, PATCH])
        vec_raw = sb("vec_raw", [8, P])
        wih_raw = sb("wih_raw", [P, KH, P])
        whh_raw = sb("whh_raw", [P, KH, HID])
        wout_raw = sb("wout_raw", [P, HID])
        fc1_raw = sb("fc1_raw", [P, E, P])
        fc2_raw = sb("fc2_raw", [P, E, P])
        gate_raw = sb("gate_raw", [ER, P])
        lorab_raw = sb("lorab_raw", [E * R, P])
        lora_a_sb = sb("lora_a_sb", [P, E, ER])
        tokw_t = sb("tokw_t", [PATCH, P])
        vecs = sb("vecs", [P, 8])
        bias_h = sb("bias_h", [P, KH])
        wih_t = sb("wih_t", [P, KH * P])
        whh_t = sb("whh_t", [P, KH * KH * P])
        wout_t = sb("wout_t", [P, KH * P])
        fc1_t = sb("fc1_t", [P, E * P])
        fc2_t = sb("fc2_t", [P, E * P])
        gate_t = sb("gate_t", [P, ER])
        lorab_t = sb("lorab_t", [P, E, ER])
        adapt = sb("adapt", [P, P])

        x_sb = sb("x_sb", [P, (STEPS + CONTEXT - 1) * D])
        x_piece = sb("x_piece", [P, 2, XW])
        patch_t = sb("patch_t", [PATCH, 2, W])
        y_sb = sb("y_sb", [P, GROUPS * W])
        bn_st = sb("bn_st", [P, GROUPS + 1, 6])
        bn_mv = sb("bn_mv", [P, 2])
        bn_tmp = sb("bn_tmp", [P, 2])
        bn_ab = sb("bn_ab", [P, 3])
        half_neg = sb("half_neg", [P, G])
        hb = sb("hb", [P, 2, W])
        ln_st = sb("ln_st", [P, 2, G, 6])
        ln_mv = sb("ln_mv", [P, 2, G, 2])
        ln_ve = sb("ln_ve", [P, 2, G])
        ln_rs = sb("ln_rs", [P, 2, G])
        z_sb = sb("z_sb", [P, 2, W])
        h_tok = sb("h_tok", [P, GROUPS * W])
        a_in = sb("a_in", [P, GROUPS * W])
        state = sb("state", [P, KH, STEPS + 1, P])

        h_feat = sb("h_feat", [P, W])
        z_feat = sb("z_feat", [P, W])
        logit_f = sb("logit_f", [P, P])
        g_in = sb("g_in", [P, G, E + 1])
        g_exp = sb("g_exp", [P, G, E + 1])
        g_max = sb("g_max", [P, G])
        g_den = sb("g_den", [P, 2, G])
        g_inv = sb("g_inv", [P, 2, G])
        g_p = sb("g_p", [P, G, E])
        g_w = sb("g_w", [P, G, E])
        g_wr = sb("g_wr", [P, G, E])
        g_sum = sb("g_sum", [P, G])
        g_sum1 = sb("g_sum1", [P, G])
        g_ws = sb("g_ws", [P, G])
        w_wide = sb("w_wide", [P, G, E, ER])
        w_feat = sb("w_feat", [P, W])
        hidden = sb("hidden", [P, E, W])
        low = sb("low", [P, W])
        o_sb = sb("o_sb", [P, W])

        diff = sb("diff", [P, KH, P])
        cmp_col = sb("cmp_col", [P, 4])
        ok_row = sb("ok_row", [1, P])
        ok_f = sb("ok_f", [1, 1])
        ok_i = sb("ok_i", [1, 1], I32)

        bank = [ctx.enter_context(nc.psum_tensor(f"bank{i}", [P, W], F32)) for i in range(8)]

        names = """ident_zero ident_made x_landed x_landed2 w_landed rnn_landed ffn_landed zeroed x_zeroed
            prep_done prep_copied adapt_done
            piece_ready patch_done patch_copied y_done y_ready bn_stats_done bn_step bn_pool
            hb_ready h_done h_kept ln_mv_ready ln_step z_ready z_done a_ready
            pre0 pre1 state0 state1
            diff_done diff_turned cmp_step cmp_turned ok_ready
            redo_pre redo_state
            wout_done hf_ready h2_done h2_ready h2_stats mv2_ready ln2_step z2_ready z2_done zf_ready
            gate_sum gate_done logit_ready logit_turned gate_step exp_ready w_ready w_turned wf_ready
            fc1_done hidden_act hidden_dve low_done low_ready mix_done out_ready stored"""
        S = {n: sem(n) for n in names.split()}

        def wait_past(eng, name, value):
            if not (isinstance(value, int) and value == 0):
                eng.wait_ge(S[name], value)

        def wait_apart(eng, name, value):
            eng.wait_ge(S[name], value)
            eng.nop(nofuse=True)

        rb = [[bank[0], bank[1]], [bank[2], bank[3]]]
        block = ctx.enter_context(nc.Block())

        prep = [
            [(tokw_raw[:, :], P, PATCH), (vec_raw[:, :], 8, P)],
            [(wih_raw[:, m, :], P, P) for m in range(KH)],
            [(whh_raw[:, m, k * P:(k + 1) * P], P, P) for m in range(KH) for k in range(KH)],
            [(wout_raw[:, k * P:(k + 1) * P], P, P) for k in range(KH)]
            + [(gate_raw[:, :], ER, P), (lorab_raw[:, :], E * R, P)],
            [(fc1_raw[:, e, :], P, P) for e in range(E)],
            [(fc2_raw[:, e, :], P, P) for e in range(E)],
        ]
        PREP_LOADS = [("w_landed", 7), ("rnn_landed", 2), ("rnn_landed", 2), ("ffn_landed", 7),
                      ("ffn_landed", 7), ("ffn_landed", 7)]
        N_PREP = len(prep)

        @block.sync
        def _(sp):
            rows = STEPS + CONTEXT - 1
            early = (2 * G + CONTEXT - 1) * D

            def x_rows(a, b):
                sp.dma_start(x_sb[0:COLS, a:b], bass.AP(tensor=x.tensor, offset=a,
                             ap=[[STEPS * D, CHUNKS - 1], [T * D, B], [1, b - a]]))\
                    .then_inc(S["x_landed" if a == 0 else "x_landed2"], 16)

            x_rows(0, early)
            sp.dma_start(tokw_raw[:, :], tok_w).then_inc(S["w_landed"], 16)
            for r, v in ((0, tok_b), (1, tok_gamma), (2, tok_beta), (3, b_out)):
                sp.dma_start(vec_raw[r:r + 1, :], v.rearrange("(a d) -> a d", a=1)).then_inc(S["w_landed"], 16)
            sp.wait_ge(S["x_zeroed"], 1)
            sp.dma_start(x_sb[COLS:P, 0:(LAST + CONTEXT - 1) * D],
                         bass.AP(tensor=x.tensor, offset=(CHUNKS - 1) * STEPS * D,
                                 ap=[[T * D, B], [1, (LAST + CONTEXT - 1) * D]])).then_inc(S["x_landed"], 16)
            x_rows(early, rows * D)
            sp.dma_start(fc1_raw[:, :, :], fc1_w.rearrange("e h i -> h e i")).then_inc(S["ffn_landed"], 16)
            sp.dma_start(fc2_raw[:, :, :], fc2_w.rearrange("e d o -> d e o")).then_inc(S["ffn_landed"], 16)
            sp.wait_ge(S["zeroed"], 1)
            sp.dma_start(lora_a_sb[:, :, 0:R], lora_a.rearrange("e h r -> h e r")).then_inc(S["ffn_landed"], 16)
            sp.dma_start(lorab_raw[:, :], lora_b.rearrange("e r o -> (e r) o")).then_inc(S["ffn_landed"], 16)

            def store(c0, n_chunks, g, steps):
                sp.dma_start(
                    bass.AP(tensor=out.tensor, offset=(c0 * STEPS + G * g) * P,
                            ap=[[STEPS * P, n_chunks], [L * P, B], [1, steps * P]]),
                    o_sb[c0 * B:(c0 + n_chunks) * B, 0:steps * P]).then_inc(S["stored"], 16)

            with sp.Fori(0, FULL) as g:
                sp.wait_ge(S["out_ready"], g + 1)
                store(0, CHUNKS, g, G)
            sp.wait_ge(S["out_ready"], FULL + 1)
            store(0, CHUNKS - 1, FULL, G)
            store(CHUNKS - 1, 1, FULL, CUT)
            with sp.Fori(FULL + 1, GROUPS) as g:
                sp.wait_ge(S["out_ready"], g + 1)
                store(0, CHUNKS - 1, g, G)
            sp.wait_ge(S["stored"], 16 * (GROUPS + 1))

        @block.gpsimd
        def _(pool):
            nc.gpsimd.memset(ident[:, :], 0.0).then_inc(S["ident_zero"], 1)
            pool.wait_ge(S["ident_zero"], 1)
            nc.gpsimd.affine_select(out=ident[:, :], in_=ident[:, :], compare_op=ALU.not_equal, fill=1.0,
                                    base=0, pattern=[[-1, P]], channel_multiplier=1).then_inc(S["ident_made"], 1)
            nc.gpsimd.memset(half_neg[:, :], -0.5)
            pool.wait_ge(S["x_landed"], 32)

            def piece(g, half):
                nc.gpsimd.tensor_copy(x_piece[:, half, :], x_sb[:, bass.ds(g * (G * D), XW)])\
                    .then_inc(S["piece_ready"], 1)

            piece(0, 0)
            piece(1, 1)
            pool.wait_ge(S["x_landed2"], 16)
            with pool.Fori(1, GROUPS // 2) as p:
                for half in range(2):
                    pool.wait_ge(S["patch_done"], 2 * p + (half - 1))
                    piece(2 * p + half, half)

            pool.wait_ge(S["bn_step"], 1)
            nc.gpsimd.tensor_scalar(bn_tmp[:, 0:1], bn_mv[:, 1:2], EPS, None, ALU.add).then_inc(S["bn_pool"], 1)
            pool.wait_ge(S["bn_pool"], 1)
            nc.gpsimd.tensor_tensor(bn_tmp[:, 1:2], bn_tmp[:, 0:1], half_neg[:, 0:1], ALU.pow)\
                .then_inc(S["bn_pool"], 1)

            with pool.Fori(0, GROUPS // 2) as q:
                gp = (q + GROUPS // 4) % (GROUPS // 2)
                for half in range(2):
                    wait_apart(pool, "ln_mv_ready", 2 * q + half + 1)
                    nc.gpsimd.tensor_scalar(ln_ve[:, half, :], ln_mv[:, half, :, 1], EPS, None, ALU.add)\
                        .then_inc(S["ln_step"], 1)
                    pool.wait_ge(S["ln_step"], 4 * q + 2 * half + 1)
                    nc.gpsimd.tensor_tensor(ln_rs[:, half, :], ln_ve[:, half, :], half_neg[:, :], ALU.pow)\
                        .then_inc(S["ln_step"], 1)

            def stage_pool(g):
                wait_apart(pool, "mv2_ready", g + 1)
                nc.gpsimd.tensor_scalar(ln_ve[:, 0, :], ln_mv[:, 0, :, 1], EPS, None, ALU.add)\
                    .then_inc(S["ln2_step"], 1)
                pool.wait_ge(S["ln2_step"], 2 * g + 1)
                nc.gpsimd.tensor_tensor(ln_rs[:, 0, :], ln_ve[:, 0, :], half_neg[:, :], ALU.pow)\
                    .then_inc(S["ln2_step"], 1)
                pool.wait_ge(S["gate_step"], 10 * g + 10)
                if not isinstance(g, int):
                    wait_apart(pool, "w_turned", g)
                for j in range(G):
                    last = nc.gpsimd.tensor_scalar(
                        w_wide[:, j, :, :], g_wr[:, j, :].unsqueeze(2).to_broadcast([P, E, ER]),
                        g_ws[:, j:j + 1], None, ALU.mult)
                last.then_inc(S["w_ready"], 1)

            stage_pool(0)
            with pool.Fori(1, GROUPS) as g:
                stage_pool(g)

        @block.scalar
        def _(act):
            for r, v in ((4, b_ih), (6, b_hh)):
                act.dma_start(vec_raw[r:r + 2, :], v.rearrange("(m h) -> m h", m=KH))\
                    .then_inc(S["w_landed"], 16)
            act.dma_start(wih_raw[:, :, :], w_ih.rearrange("(m h) i -> h m i", m=KH)).then_inc(S["rnn_landed"], 16)
            act.dma_start(whh_raw[:, :, :], w_hh.rearrange("(m h) i -> h m i", m=KH)).then_inc(S["rnn_landed"], 16)
            act.dma_start(wout_raw[:, :], w_out).then_inc(S["ffn_landed"], 16)
            act.wait_ge(S["zeroed"], 1)
            act.dma_start(gate_raw[0:E, :], gate_w).then_inc(S["ffn_landed"], 16)
            act.dma_start(gate_raw[E:E + 1, :], thr_w).then_inc(S["ffn_landed"], 16)

            def copied(dst, src):
                return nc.scalar.activation(dst, src, ACT.Copy)

            act.wait_ge(S["prep_done"], 1)
            copied(tokw_t[:, :], bank[0][0:PATCH, 0:P])
            copied(vecs[:, :], bank[0][:, P:P + 8]).then_inc(S["prep_copied"], 1)

            act.wait_ge(S["prep_copied"], 1)
            with act.Fori(0, GROUPS // 2) as p:
                for half in range(2):
                    act.wait_ge(S["y_done"], 2 * p + half + 1)
                    nc.scalar.activation(y_sb[:, bass.ds((2 * p + half) * W, W)], bank[6 + half][:, :],
                                         ACT.Relu, bias=vecs[:, 0:1]).then_inc(S["y_ready"], 1)

            act.wait_ge(S["prep_done"], 2)
            copied(wih_t[:, :], bank[1][:, 0:KH * P]).then_inc(S["prep_copied"], 1)
            act.wait_ge(S["prep_done"], 3)
            copied(whh_t[:, :], bank[2][:, :]).then_inc(S["prep_copied"], 1)
            act.wait_ge(S["prep_done"], 4)
            copied(wout_t[:, :], bank[3][:, 0:KH * P])
            copied(gate_t[:, :], bank[3][:, 2 * P:2 * P + ER])
            act.wait_ge(S["zeroed"], 1)
            copied(lorab_t[:, :, 0:R], bank[3][:, 3 * P:3 * P + E * R].rearrange("p (e r) -> p e r", e=E))\
                .then_inc(S["prep_copied"], 1)
            act.wait_ge(S["prep_done"], 5)
            copied(fc1_t[:, :], bank[4][:, :]).then_inc(S["prep_copied"], 1)
            act.wait_ge(S["prep_done"], 6)
            copied(fc2_t[:, :], bank[5][:, :]).then_inc(S["prep_copied"], 1)
            act.wait_ge(S["prep_done"], 7)
            copied(adapt[:, :], bank[6][:, 0:P]).then_inc(S["adapt_done"], 1)

            def bn_apply(g, half):
                nc.scalar.activation(hb[:, half, :], y_sb[:, bass.ds(g * W, W)], ACT.Identity,
                                     bias=bn_ab[:, 2:3], scale=bn_ab[:, 0:1]).then_inc(S["hb_ready"], 1)

            act.wait_ge(S["bn_step"], 4)

            def ln1_a(q, half, again):
                gp = (q + GROUPS // 4) % (GROUPS // 2)
                if again:
                    act.wait_ge(S["h_done"], 2 * q + half - 1)
                bn_apply(2 * gp + half, half)

            def ln1_b(q, half):
                gp = (q + GROUPS // 4) % (GROUPS // 2)
                act.wait_ge(S["z_done"], 2 * q + half + 1)
                copied(a_in[:, bass.ds((2 * gp + half) * W, W)], bank[6 + half][:, :]).then_inc(S["a_ready"], 1)

            def relu1(n, slot, a, src0, src1):
                act.wait_ge(S["pre1"], n + 1)
                nc.scalar.activation(state[:, 1, slot, a:a + src1], rb[1][src0][:, 0:src1], ACT.Relu,
                                     bias=bias_h[:, 1:2]).then_inc(S["state1"], 1)

            ln1_a(0, 0, False)
            ln1_a(0, 1, False)
            ln1_b(0, 0)
            ln1_b(0, 1)
            with act.Fori(0, WARM // G) as i:
                ln1_a(i + 1, 0, True)
                relu1(G * i, 1, B, 0, COLS)
                ln1_a(i + 1, 1, True)
                relu1(G * i + 1, 0, B, 1, COLS)
                relu1(G * i + 2, 1, B, 0, COLS)
                ln1_b(i + 1, 0)
                relu1(G * i + 3, 0, B, 1, COLS)
                ln1_b(i + 1, 1)
            with act.Fori(0, GROUPS) as g:
                for j in range(G):
                    relu1(WARM + G * g + j, bass.ds(G * g + j + 1, 1), 0, j % 2, P)

            def stage1(g):
                act.wait_ge(S["wout_done"], g + 1)
                wait_past(act, "h2_done", g)
                nc.scalar.activation(h_feat[:, :], bank[0][:, :], ACT.Identity, bias=vecs[:, 3:4])\
                    .then_inc(S["hf_ready"], 1)

            def stage1b(g):
                act.wait_ge(S["z2_done"], g + 1)
                wait_past(act, "fc1_done", E * g)
                copied(z_feat[:, :], bank[2][:, :]).then_inc(S["zf_ready"], 1)

            def stage2(g, more):
                act.wait_ge(S["gate_done"], g + 1)
                copied(logit_f[:, :], bank[3][:, 0:P]).then_inc(S["logit_ready"], 1)
                act.wait_ge(S["fc1_done"], E * g + 1)
                wait_past(act, "low_done", g)
                nc.scalar.activation(hidden[:, 0, :], bank[4][:, :], ACT.Relu).then_inc(S["hidden_act"], 1)
                if more:
                    stage1(g + 1)
                act.wait_ge(S["gate_step"], 10 * g + 3)
                nc.scalar.activation(g_exp[:, :, :], g_in[:, :, :], ACT.Exp).then_inc(S["exp_ready"], 1)
                act.wait_ge(S["fc1_done"], E * g + 3)
                nc.scalar.activation(hidden[:, 2, :], bank[4][:, :], ACT.Relu).then_inc(S["hidden_act"], 1)
                act.wait_ge(S["fc1_done"], E * g + 4)
                nc.scalar.activation(hidden[:, 3, :], bank[5][:, :], ACT.Relu).then_inc(S["hidden_act"], 1)
                act.wait_ge(S["w_turned"], g + 1)
                wait_past(act, "low_ready", g)
                copied(w_feat[:, :], bank[3][:, :]).then_inc(S["wf_ready"], 1)
                if more:
                    stage1b(g + 1)

            stage1(0)
            stage1b(0)
            stage2(0, True)
            with act.Fori(1, GROUPS - 1) as g:
                stage2(g, True)
            stage2(GROUPS - 1, False)

        @block.vector
        def _(dve):
            tail_cols = (LAST + CONTEXT - 1) * D
            nc.vector.memset(x_sb[96:P, tail_cols:], 0.0).then_inc(S["x_zeroed"], 1)
            nc.vector.memset(gate_raw[:, :], 0.0)
            nc.vector.memset(lora_a_sb[:, :, :], 0.0)
            nc.vector.memset(state[:, 0, 0:2, :], 0.0).then_inc(S["state0"], 1)
            nc.vector.memset(state[:, 1, 0:2, :], 0.0).then_inc(S["state1"], 1)
            nc.vector.memset(lorab_t[:, :, :], 0.0).then_inc(S["zeroed"], 1)

            def patch_copy(g, half, again):
                dve.wait_ge(S["patch_done"], g + 1)
                if again:
                    dve.wait_ge(S["y_done"], g - 1)
                nc.vector.tensor_copy(patch_t[:, half, :], bank[4 + half][0:PATCH, :])\
                    .then_inc(S["patch_copied"], 1)

            def stats(g, kind):
                wait_apart(dve, "y_ready", g + 1)
                if kind == "full":
                    nc.vector.bn_stats(bn_st[:, bass.ds(g, 1), :], y_sb[:, bass.ds(g * W, W)])\
                        .then_inc(S["bn_stats_done"], 1)
                elif kind == "short":
                    v = y_sb[:, bass.ds(g * W, W)].rearrange("p (j c) -> p j c", j=G)
                    nc.vector.bn_stats(bn_st[:, bass.ds(g, 1), :], v[:, :, 0:COLS])\
                        .then_inc(S["bn_stats_done"], 1)
                else:
                    v = y_sb[:, g * W:(g + 1) * W].rearrange("p (j c) -> p j c", j=G)
                    nc.vector.bn_stats(bn_st[:, g, :], y_sb[:, g * W:g * W + CUT * P])
                    nc.vector.bn_stats(bn_st[:, GROUPS, :], v[:, CUT:G, 0:COLS]).then_inc(S["bn_stats_done"], 1)

            patch_copy(0, 0, False)
            patch_copy(1, 1, False)
            stats(0, "full")
            with dve.Fori(1, FULL // 2) as p:
                patch_copy(2 * p, 0, True)
                stats(2 * p - 1, "full")
                patch_copy(2 * p + 1, 1, True)
                stats(2 * p, "full")
            patch_copy(FULL, 0, True)
            stats(FULL - 1, "full")
            patch_copy(FULL + 1, 1, True)
            stats(FULL, "cut")
            with dve.Fori(FULL // 2 + 1, GROUPS // 2) as p:
                patch_copy(2 * p, 0, True)
                stats(2 * p - 1, "short")
                patch_copy(2 * p + 1, 1, True)
                stats(2 * p, "short")
            stats(GROUPS - 1, "short")

            dve.wait_ge(S["bn_stats_done"], GROUPS)
            nc.vector.bn_aggr(bn_mv[:, :], bn_st[:, :, :]).then_inc(S["bn_step"], 1)
            dve.wait_ge(S["prep_copied"], 1)
            nc.vector.tensor_tensor(bias_h[:, :], vecs[:, 4:6], vecs[:, 6:8], ALU.add)
            dve.wait_ge(S["bn_pool"], 2)
            nc.vector.tensor_tensor(bn_ab[:, 0:1], vecs[:, 1:2], bn_tmp[:, 1:2], ALU.mult).then_inc(S["bn_step"], 1)
            dve.wait_ge(S["bn_step"], 2)
            nc.vector.tensor_tensor(bn_ab[:, 1:2], bn_mv[:, 0:1], bn_ab[:, 0:1], ALU.mult).then_inc(S["bn_step"], 1)
            dve.wait_ge(S["bn_step"], 3)
            nc.vector.tensor_tensor(bn_ab[:, 2:3], vecs[:, 2:3], bn_ab[:, 1:2], ALU.subtract)\
                .then_inc(S["bn_step"], 1)

            def ln1_stats(q, half):
                gp = (q + GROUPS // 4) % (GROUPS // 2)
                dve.wait_ge(S["h_done"], 2 * q + half + 1)
                for j in range(G):
                    nc.vector.bn_stats(ln_st[:, half, j, :], bank[4 + half][:, j * P:(j + 1) * P])
                nc.vector.tensor_copy(h_tok[:, bass.ds((2 * gp + half) * W, W)], bank[4 + half][:, :])\
                    .then_inc(S["h_kept"], 1)
                wait_apart(dve, "h_kept", 2 * q + half + 1)
                for j in range(G):
                    last = nc.vector.bn_aggr(ln_mv[:, half, j, :], ln_st[:, half, j, :])
                last.then_inc(S["ln_mv_ready"], 1)

            def ln1_norm(q, half, again):
                gp = (q + GROUPS // 4) % (GROUPS // 2)
                dve.wait_ge(S["ln_step"], 4 * q + 2 * half + 2)
                if again:
                    dve.wait_ge(S["z_done"], 2 * q + half - 1)
                for j in range(G):
                    last = nc.vector.tensor_scalar(
                        z_sb[:, half, j * P:(j + 1) * P],
                        h_tok[:, bass.ds((2 * gp + half) * W + j * P, P)],
                        ln_mv[:, half, j, 0:1], ln_rs[:, half, j:j + 1], ALU.subtract, ALU.mult)
                last.then_inc(S["z_ready"], 1)

            def relu0(n, slot, a, parity, cols):
                dve.wait_ge(S["pre0"], n + 1)
                nc.vector.tensor_scalar(state[:, 0, slot, a:a + cols], rb[0][parity][:, 0:cols],
                                        bias_h[:, 0:1], 0.0, ALU.add, ALU.max).then_inc(S["state0"], 1)

            ln1_stats(0, 0)
            ln1_stats(0, 1)
            ln1_norm(0, 0, False)
            ln1_norm(0, 1, False)
            with dve.Fori(0, WARM // G) as i:
                relu0(G * i, 1, B, 0, COLS)
                ln1_stats(i + 1, 0)
                relu0(G * i + 1, 0, B, 1, COLS)
                ln1_stats(i + 1, 1)
                relu0(G * i + 2, 1, B, 0, COLS)
                ln1_norm(i + 1, 0, True)
                relu0(G * i + 3, 0, B, 1, COLS)
                ln1_norm(i + 1, 1, True)
            with dve.Fori(0, GROUPS) as g:
                for j in range(G):
                    relu0(WARM + G * g + j, bass.ds(G * g + j + 1, 1), 0, j % 2, P)

            dve.wait_ge(S["state0"], WARM + STEPS + 1)
            dve.wait_ge(S["state1"], WARM + STEPS + 1)
            nc.vector.tensor_tensor(diff[:, :, 0:COLS], state[:, :, 0, B:P], state[:, :, STEPS, 0:COLS],
                                    ALU.subtract).then_inc(S["diff_done"], 1)
            dve.wait_ge(S["diff_turned"], 1)
            turned = [bank[i][0:COLS, 0:KH * P] for i in (4, 5)]
            nc.vector.tensor_reduce(cmp_col[0:COLS, 0:1], turned[0], AX_X, ALU.max)
            nc.vector.tensor_reduce(cmp_col[0:COLS, 1:2], turned[0], AX_X, ALU.min)
            nc.vector.tensor_reduce(cmp_col[0:COLS, 2:3], turned[1], AX_X, ALU.max).then_inc(S["cmp_step"], 1)
            dve.wait_ge(S["cmp_step"], 1)
            nc.vector.scalar_tensor_tensor(cmp_col[0:COLS, 3:4], cmp_col[0:COLS, 1:2], -1.0,
                                           cmp_col[0:COLS, 0:1], ALU.mult, ALU.max).then_inc(S["cmp_step"], 1)
            dve.wait_ge(S["cmp_step"], 2)
            nc.vector.scalar_tensor_tensor(diff[0:COLS, 0, 0:1], cmp_col[0:COLS, 2:3], TOL,
                                           cmp_col[0:COLS, 3:4], ALU.mult, ALU.is_ge).then_inc(S["cmp_step"], 1)
            dve.wait_ge(S["cmp_turned"], 1)
            nc.vector.tensor_reduce(ok_f[:, :], bank[6][0:1, 0:COLS], AX_X, ALU.min).then_inc(S["cmp_step"], 1)
            dve.wait_ge(S["cmp_step"], 4)
            nc.vector.tensor_copy(ok_i[:, :], ok_f[:, :]).then_inc(S["ok_ready"], 1)
            dve.wait_ge(S["ok_ready"], 1)
            ok = dve.value_load(ok_i[0:1, 0:1], min_val=0, max_val=1)
            with dve.If(ok == 0):
                def redo_step(n, s, col):
                    dve.wait_ge(S["redo_pre"], n + 1)
                    for m in range(KH):
                        last = nc.vector.tensor_scalar(
                            state[:, m, bass.ds(s + 1, 1), bass.ds(col, B)], bank[m][:, 0:B],
                            bias_h[:, m:m + 1], 0.0, ALU.add, ALU.max)
                    last.then_inc(S["redo_state"], 1)

                nc.vector.memset(state[:, :, 0, 0:B], 0.0).then_inc(S["redo_state"], 1)
                with dve.Fori(0, CHUNKS - 1) as c:
                    with dve.Fori(0, STEPS) as s:
                        redo_step(c * STEPS + s, s, c * B)
                    dve.wait_ge(S["redo_state"], (c + 1) * (STEPS + 1))
                    nc.vector.tensor_copy(state[:, :, 0, bass.ds(c * B + B, B)],
                                          state[:, :, STEPS, bass.ds(c * B, B)]).then_inc(S["redo_state"], 1)
                with dve.Fori(0, STEPS) as s:
                    redo_step((CHUNKS - 1) * STEPS + s, s, COLS)
            dve.end_ifs()

            def stage1(g):
                dve.wait_ge(S["h2_done"], g + 1)
                nc.vector.tensor_tensor(h_tok[:, bass.ds(g * W, W)], bank[1][:, :],
                                        h_tok[:, bass.ds(g * W, W)], ALU.add).then_inc(S["h2_ready"], 1)
                wait_apart(dve, "h2_ready", g + 1)
                for j in range(G):
                    last = nc.vector.bn_stats(ln_st[:, 0, j, :], h_tok[:, bass.ds(g * W + j * P, P)])
                last.then_inc(S["h2_stats"], 1)
                wait_apart(dve, "h2_stats", g + 1)
                for j in range(G):
                    last = nc.vector.bn_aggr(ln_mv[:, 0, j, :], ln_st[:, 0, j, :])
                last.then_inc(S["mv2_ready"], 1)

            def stage1b(g):
                dve.wait_ge(S["ln2_step"], 2 * g + 2)
                wait_past(dve, "z2_done", g)
                for j in range(G):
                    last = nc.vector.tensor_scalar(
                        z_sb[:, 0, j * P:(j + 1) * P], h_tok[:, bass.ds(g * W + j * P, P)],
                        ln_mv[:, 0, j, 0:1], ln_rs[:, 0, j:j + 1], ALU.subtract, ALU.mult)
                last.then_inc(S["z2_ready"], 1)

            def bc(v, n):
                return v.unsqueeze(2).to_broadcast([P, G, n])

            def gates(g):
                k = 10 * g

                def step(n, instr):
                    instr.then_inc(S["gate_step"], 1)
                    dve.wait_ge(S["gate_step"], k + n)

                dve.wait_ge(S["logit_turned"], g + 1)
                lg = bank[3][:, P:2 * P].rearrange("p (j c) -> p j c", j=G)
                step(1, nc.vector.tensor_reduce(g_max[:, :], lg[:, :, 0:E], AX_X, ALU.max))
                step(2, nc.vector.tensor_tensor(g_in[:, :, 0:E], lg[:, :, 0:E], bc(g_max[:, :], E), ALU.subtract))
                nc.vector.tensor_scalar(g_in[:, :, E], lg[:, :, E], -1.0, None, ALU.mult).then_inc(S["gate_step"], 1)

            def gates_b(g):
                k = 10 * g

                def step(n, instr):
                    instr.then_inc(S["gate_step"], 1)
                    dve.wait_ge(S["gate_step"], k + n)

                dve.wait_ge(S["exp_ready"], g + 1)
                nc.vector.tensor_reduce(g_den[:, 0, :], g_exp[:, :, 0:E], AX_X, ALU.add)
                step(4, nc.vector.tensor_scalar(g_den[:, 1, :], g_exp[:, :, E], float(E), float(E),
                                                ALU.mult, ALU.add))
                step(5, nc.vector.reciprocal(g_inv[:, :, :], g_den[:, :, :]))
                step(6, nc.vector.tensor_tensor(g_p[:, :, :], g_exp[:, :, 0:E], bc(g_inv[:, 0, :], E), ALU.mult))
                step(7, nc.vector.tensor_tensor(g_w[:, :, :], g_p[:, :, :], bc(g_inv[:, 1, :], E), ALU.subtract))
                step(8, nc.vector.tensor_scalar(g_wr[:, :, :], g_w[:, :, :], 0.0, None, ALU.max))
                nc.vector.tensor_reduce(g_sum[:, :], g_wr[:, :, :], AX_X, ALU.add).then_inc(S["gate_sum"], 1)
                dve.wait_ge(S["gate_sum"], 2 * g + 1)
                nc.vector.scalar_tensor_tensor(g_sum1[:, :], g_sum[:, :], 0.0, g_sum[:, :],
                                               ALU.is_equal, ALU.add).then_inc(S["gate_sum"], 1)
                dve.wait_ge(S["gate_sum"], 2 * g + 2)
                nc.vector.reciprocal(g_ws[:, :], g_sum1[:, :]).then_inc(S["gate_step"], 2)

            def stage2(g, more, stores):
                gates(g)
                dve.wait_ge(S["fc1_done"], E * g + 2)
                wait_past(dve, "low_done", g)
                nc.vector.tensor_scalar(hidden[:, 1, :], bank[5][:, :], 0.0, None, ALU.max)\
                    .then_inc(S["hidden_dve"], 1)
                gates_b(g)
                if more:
                    stage1(g + 1)
                    stage1b(g + 1)
                dve.wait_ge(S["wf_ready"], g + 1)
                dve.wait_ge(S["low_done"], g + 1)
                wait_past(dve, "mix_done", g)
                nc.vector.tensor_tensor(low[:, :], bank[6][:, :], w_feat[:, :], ALU.mult).then_inc(S["low_ready"], 1)
                dve.wait_ge(S["mix_done"], g + 1)
                wait_past(dve, "stored", 16 * (g + stores))
                nc.vector.tensor_tensor(o_sb[:, :], bank[7][:, :], h_tok[:, bass.ds(g * W, W)], ALU.add)\
                    .then_inc(S["out_ready"], 1)

            stage1(0)
            stage1b(0)
            stage2(0, True, 0)
            with dve.Fori(1, FULL + 1) as g:
                stage2(g, True, 0)
            with dve.Fori(FULL + 1, GROUPS - 1) as g:
                stage2(g, True, 1)
            stage2(GROUPS - 1, False, 1)

        @block.tensor
        def _(pe):
            def turn(b, n):
                name, loads = PREP_LOADS[n]
                pe.wait_ge(S[name], 16 * loads)
                for i, (src, rows, cols) in enumerate(prep[n]):
                    last = nc.tensor.transpose(bank[b][0:cols, i * P:i * P + rows], src, ident[0:rows, 0:rows])
                last.then_inc(S["prep_done"], 1)

            pe.wait_ge(S["ident_made"], 1)
            turn(0, 0)

            def patches(g, half, again):
                pe.wait_ge(S["piece_ready"], g + 1)
                if again:
                    pe.wait_ge(S["patch_copied"], g - 1)
                for j in range(G):
                    last = nc.tensor.transpose(bank[4 + half][0:PATCH, j * P:(j + 1) * P],
                                               x_piece[:, half, j * D:j * D + PATCH], ident[:, :])
                last.then_inc(S["patch_done"], 1)

            def tdnn(g, half, again):
                pe.wait_ge(S["patch_copied"], g + 1)
                if again:
                    pe.wait_ge(S["y_ready"], g - 1)
                nc.tensor.matmul(bank[6 + half][:, :], tokw_t[:, :], patch_t[:, half, :], start=True, stop=True)\
                    .then_inc(S["y_done"], 1)

            patches(0, 0, False)
            patches(1, 1, False)
            pe.wait_ge(S["prep_copied"], 1)
            tdnn(0, 0, False)
            patches(2, 0, True)
            tdnn(1, 1, False)
            patches(3, 1, True)
            tdnn(2, 0, True)
            with pe.Fori(2, GROUPS // 2) as p:
                patches(2 * p, 0, True)
                tdnn(2 * p - 1, 1, True)
                patches(2 * p + 1, 1, True)
                tdnn(2 * p, 0, True)
            tdnn(GROUPS - 1, 1, True)

            for n in range(1, N_PREP):
                if n == 4:
                    pe.wait_ge(S["patch_copied"], GROUPS)
                turn(n, n)
            pe.wait_ge(S["prep_copied"], N_PREP)
            pe.wait_ge(S["y_ready"], GROUPS)
            for e in range(E):
                last = nc.tensor.matmul(bank[6][ER * e:ER * (e + 1), 0:P], lorab_t[:, e, :],
                                        fc2_t[:, e * P:(e + 1) * P], start=True, stop=True)
            last.then_inc(S["prep_done"], 1)
            pe.wait_ge(S["adapt_done"], 1)

            def ln1_turn(q, half, again):
                pe.wait_ge(S["hb_ready"], 2 * q + half + 1)
                if again:
                    pe.wait_ge(S["h_kept"], 2 * q + half - 1)
                for j in range(G):
                    last = nc.tensor.transpose(bank[4 + half][:, j * P:(j + 1) * P],
                                               hb[:, half, j * P:(j + 1) * P], ident[:, :])
                last.then_inc(S["h_done"], 1)

            def ln1_back(q, half, again):
                pe.wait_ge(S["z_ready"], 2 * q + half + 1)
                if again:
                    pe.wait_ge(S["a_ready"], 2 * q + half - 1)
                for j in range(G):
                    last = nc.tensor.transpose(bank[6 + half][:, j * P:(j + 1) * P],
                                               z_sb[:, half, j * P:(j + 1) * P], ident[:, :])
                last.then_inc(S["z_done"], 1)

            def project(parity, col, cols):
                for m in range(KH):
                    nc.tensor.matmul(rb[m][parity][:, 0:cols], wih_t[:, m * P:(m + 1) * P],
                                     a_in[:, bass.ds(col, cols)], start=True, stop=False)

            def recur(n, parity, rhs, cols):
                for k in range(KH):
                    pe.wait_ge(S["state0" if k == 0 else "state1"], n + 1)
                    for m in range(KH):
                        mm = nc.tensor.matmul(rb[m][parity][:, 0:cols], whh_t[:, (m * KH + k) * P:(m * KH + k + 1) * P],
                                              rhs(k), start=False, stop=(k == KH - 1))
                        if k == KH - 1:
                            mm.then_inc(S["pre0" if m == 0 else "pre1"], 1)

            ln1_turn(0, 0, False)
            ln1_turn(0, 1, False)
            ln1_back(0, 0, False)
            ln1_back(0, 1, False)
            pe.wait_ge(S["a_ready"], 2)
            WARM_COL = (STEPS - WARM) * P
            project(0, WARM_COL, COLS)
            pe.wait_ge(S["zeroed"], 1)
            with pe.Fori(0, WARM // G - 1) as i:
                for j in range(G):
                    recur(G * i + j, j % 2, lambda k: state[:, k, j % 2, B:P], COLS)
                    if j == G - 1:
                        pe.wait_ge(S["a_ready"], i + 3)
                    project((j + 1) % 2, WARM_COL + (G * i + j + 1) * P, COLS)
                    (ln1_turn if j < 2 else ln1_back)(i + 1, j % 2, True)
            i = WARM // G - 1
            for j in range(G):
                recur(G * i + j, j % 2, lambda k: state[:, k, j % 2, B:P], COLS)
                if j < G - 1:
                    project((j + 1) % 2, WARM_COL + (G * i + j + 1) * P, COLS)
                (ln1_turn if j < 2 else ln1_back)(i + 1, j % 2, True)
            project(0, 0, P)

            def main_steps(g, more):
                for j in range(G):
                    recur(WARM + G * g + j, j % 2, lambda k: state[:, k, bass.ds(G * g + j, 1), :], P)
                    if j < G - 1 or more:
                        if j == G - 1:
                            pe.wait_ge(S["a_ready"], GROUPS)
                        project((j + 1) % 2, (G * g + j + 1) * P, P)

            with pe.Fori(0, GROUPS - 1) as g:
                main_steps(g, True)
            main_steps(GROUPS - 1, False)

            pe.wait_ge(S["diff_done"], 1)
            for k in range(KH):
                nc.tensor.transpose(bank[4][0:COLS, k * P:(k + 1) * P], diff[:, k, 0:COLS], ident[:, :])
                last = nc.tensor.transpose(bank[5][0:COLS, k * P:(k + 1) * P], state[:, k, STEPS, 0:COLS],
                                           ident[:, :])
            last.then_inc(S["diff_turned"], 1)
            pe.wait_ge(S["cmp_step"], 3)
            nc.tensor.transpose(bank[6][0:1, 0:COLS], diff[0:COLS, 0, 0:1], ident[0:COLS, 0:COLS])\
                .then_inc(S["cmp_turned"], 1)
            pe.wait_ge(S["ok_ready"], 1)
            ok = pe.value_load(ok_i[0:1, 0:1], min_val=0, max_val=1)
            with pe.If(ok == 0):
                def redo_step(n, s, col):
                    pe.wait_ge(S["redo_state"], n)
                    for m in range(KH):
                        nc.tensor.matmul(bank[m][:, 0:B], wih_t[:, m * P:(m + 1) * P],
                                         a_in[:, bass.ds(s * P + col, B)], start=True, stop=False)
                        for k in range(KH):
                            last = nc.tensor.matmul(
                                bank[m][:, 0:B], whh_t[:, (m * KH + k) * P:(m * KH + k + 1) * P],
                                state[:, k, bass.ds(s, 1), bass.ds(col, B)], start=False, stop=(k == KH - 1))
                    last.then_inc(S["redo_pre"], 1)

                with pe.Fori(0, CHUNKS - 1) as c:
                    with pe.Fori(0, STEPS) as s:
                        redo_step(c * (STEPS + 1) + s + 1, s, c * B)
                with pe.Fori(0, STEPS) as s:
                    redo_step((CHUNKS - 1) * (STEPS + 1) + s + 1, s, COLS)
                pe.wait_ge(S["redo_state"], CHUNKS * (STEPS + 1))
            pe.end_ifs()

            def w_out_sum(g):
                wait_past(pe, "hf_ready", g)
                for k in range(KH):
                    mm = nc.tensor.matmul(bank[0][:, :], wout_t[:, k * P:(k + 1) * P],
                                          state[:, k, bass.ds(G * g + 1, G), :], start=(k == 0), stop=(k == KH - 1))
                mm.then_inc(S["wout_done"], 1)

            def turn4(dst, src, wait, value, done):
                pe.wait_ge(S[wait], value)
                for j in range(G):
                    last = nc.tensor.transpose(dst[:, j * P:(j + 1) * P], src(j), ident[:, :])
                last.then_inc(S[done], 1)

            def h_turn(g):
                wait_past(pe, "h2_ready", g)
                turn4(bank[1], lambda j: h_feat[:, j * P:(j + 1) * P], "hf_ready", g + 1, "h2_done")

            def z_turn(g):
                wait_past(pe, "zf_ready", g)
                turn4(bank[2], lambda j: z_sb[:, 0, j * P:(j + 1) * P], "z2_ready", g + 1, "z2_done")

            def fc1(g, e):
                if e == 2:
                    pe.wait_ge(S["hidden_act"], 3 * g + 1)
                elif e == 3:
                    pe.wait_ge(S["hidden_dve"], g + 1)
                elif e == 0:
                    wait_past(pe, "hidden_act", 3 * g)
                nc.tensor.matmul(bank[4 + e % 2][:, :], fc1_t[:, e * P:(e + 1) * P], z_feat[:, :],
                                 start=True, stop=True).then_inc(S["fc1_done"], 1)

            def stage2(g, more):
                pe.wait_ge(S["zf_ready"], g + 1)
                wait_past(pe, "wf_ready", g)
                for j in range(G):
                    last = nc.tensor.matmul(bank[3][ER * j:ER * (j + 1), 0:P], gate_t[:, :],
                                            z_feat[:, j * P:(j + 1) * P], start=True, stop=True)
                last.then_inc(S["gate_done"], 1)
                fc1(g, 0)
                pe.wait_ge(S["logit_ready"], g + 1)
                nc.tensor.transpose(bank[3][:, P:2 * P], logit_f[:, :], ident[:, :]).then_inc(S["logit_turned"], 1)
                fc1(g, 1)
                if more:
                    w_out_sum(g + 1)
                fc1(g, 2)
                if more:
                    h_turn(g + 1)
                fc1(g, 3)
                turn4(bank[3], lambda j: w_wide[:, j, :, :], "w_ready", g + 1, "w_turned")
                pe.wait_ge(S["hidden_act"], 3 * g + 3)
                pe.wait_ge(S["hidden_dve"], g + 1)
                wait_past(pe, "low_ready", g)
                for e in range(E):
                    last = nc.tensor.matmul(bank[6][ER * e:ER * (e + 1), :], lora_a_sb[:, e, :], hidden[:, e, :],
                                            start=True, stop=True)
                last.then_inc(S["low_done"], 1)
                if more:
                    z_turn(g + 1)
                pe.wait_ge(S["low_ready"], g + 1)
                wait_past(pe, "out_ready", g)
                for j in range(G):
                    last = nc.tensor.matmul(bank[7][:, j * P:(j + 1) * P], low[:, j * P:(j + 1) * P], adapt[:, :],
                                            start=True, stop=True)
                last.then_inc(S["mix_done"], 1)

            w_out_sum(0)
            h_turn(0)
            z_turn(0)
            stage2(0, True)
            with pe.Fori(1, GROUPS - 1) as g:
                stage2(g, True)
            stage2(GROUPS - 1, False)


_INS = ['x', 'L0_tok_W', 'L0_tok_b', 'L0_tok_gamma', 'L0_tok_beta', 'L0_attn_W_ih', 'L0_attn_W_hh',
        'L0_attn_b_ih', 'L0_attn_b_hh', 'L0_attn_W_out', 'L0_attn_b_out', 'L0_ffn_gate_w', 'L0_ffn_thr_w',
        'L0_ffn_fc1_w', 'L0_ffn_lora_A', 'L0_ffn_lora_B', 'L0_ffn_fc2_w']


def kernel(**inputs):
    import numpy as _np
    import concourse.bacc as _bacc
    from concourse import mybir as _mybir
    from concourse.bass_utils import run_bass_kernel_spmd as _run

    nc = _bacc.Bacc("TRN2", target_bir_lowering=False, num_devices=1)
    arrays, args = {}, []
    for name in _INS:
        a = _np.ascontiguousarray(inputs[name])
        arrays[f"in_{name}_dram"] = a
        args.append(nc.dram_tensor(f"in_{name}_dram", a.shape, _mybir.dt.from_np(a.dtype), kind="ExternalInput").ap())
    B, T, D = inputs['x'].shape
    O, F = inputs['L0_tok_W'].shape
    out = nc.dram_tensor("out_dram", (B, T - F // D + 1, O), _mybir.dt.float32, kind="ExternalOutput").ap()
    audio_tower(nc, *args, out)
    r = _run(nc, [arrays], core_ids=[0])
    return r.results[0]["out_dram"]
```

```python
from contextlib import ExitStack

import concourse.bass as bass
from concourse import mybir

ALU = mybir.AluOpType
ACT = mybir.ActivationFunctionType
AX_X = mybir.AxisListType.X
F32 = mybir.dt.float32
I32 = mybir.dt.int32

P = 128
EPS = 1e-5


def audio_tower(nc, x, tok_w, tok_b, tok_gamma, tok_beta, w_ih, w_hh, b_ih, b_hh, w_out, b_out,
                gate_w, thr_w, fc1_w, lora_a, lora_b, fc2_w, out):
    B, T, D = x.shape
    FEAT, PATCH = tok_w.shape
    CONTEXT = PATCH // D
    HID = w_hh.shape[0]
    KH = HID // P
    E, R = lora_a.shape[0], lora_a.shape[2]
    L = T - CONTEXT + 1
    CHUNKS = P // B
    G = 4
    STEPS = -(-L // (CHUNKS * G)) * G
    GROUPS = STEPS // G
    WARM = 20
    LAST = L - (CHUNKS - 1) * STEPS
    W = G * P
    XW = (G + CONTEXT - 1) * D
    ER = 32
    FULL = LAST // G
    CUT = LAST % G
    FIRST = GROUPS - WARM // G
    TOL = 2.0 ** -20
    assert KH == 2 and FEAT == P and E * ER == P and GROUPS % 2 == 0 and WARM % G == 0
    assert FULL % 2 == 0 and 0 < CUT < G and 2 * (WARM // G + 1) == GROUPS >= 6
    COLS = (CHUNKS - 1) * B

    with ExitStack() as ctx:
        def sb(name, shape, dt=F32):
            return ctx.enter_context(nc.sbuf_tensor(name, shape, dt))

        def sem(name):
            return ctx.enter_context(nc.semaphore(name))

        ident = sb("ident", [P, P])
        tokw_raw = sb("tokw_raw", [P, PATCH])
        vec_raw = sb("vec_raw", [8, P])
        tokb_raw = sb("tokb_raw", [1, P])
        wih_raw = sb("wih_raw", [P, KH, P])
        whh_raw = sb("whh_raw", [P, KH, HID])
        wout_raw = sb("wout_raw", [P, HID])
        fc1_raw = sb("fc1_raw", [P, E, P])
        fc2_raw = sb("fc2_raw", [P, E, P])
        gate_raw = sb("gate_raw", [ER, P])
        lorab_raw = sb("lorab_raw", [E * R, P])
        lora_a_sb = sb("lora_a_sb", [P, E, ER])
        tokw_t = sb("tokw_t", [PATCH, P])
        tok_bias = sb("tok_bias", [P, 1])
        vecs = sb("vecs", [P, 8])
        bias_h = sb("bias_h", [P, KH])
        wih_t = sb("wih_t", [P, KH * P])
        whh_t = sb("whh_t", [P, KH * KH * P])
        wout_t = sb("wout_t", [P, KH * P])
        fc1_t = sb("fc1_t", [P, E * P])
        fc2_t = sb("fc2_t", [P, E * P])
        gate_t = sb("gate_t", [P, ER])
        lorab_t = sb("lorab_t", [P, E, ER])
        adapt = sb("adapt", [P, P])

        x_sb = sb("x_sb", [P, (STEPS + CONTEXT - 1) * D])
        x_piece = sb("x_piece", [P, 2, XW])
        patch_t = sb("patch_t", [PATCH, 2, W])
        y_sb = sb("y_sb", [P, GROUPS * W])
        bn_st = sb("bn_st", [P, GROUPS + 1, 6])
        bn_mv = sb("bn_mv", [P, 2])
        bn_tmp = sb("bn_tmp", [P, 2])
        bn_ab = sb("bn_ab", [P, 3])
        half_neg = sb("half_neg", [P, G])
        hb = sb("hb", [P, 2, W])
        ln_st = sb("ln_st", [P, 2, G, 6])
        ln_mv = sb("ln_mv", [P, 2, G, 2])
        ln_ve = sb("ln_ve", [P, 2, G])
        ln_rs = sb("ln_rs", [P, 2, G])
        z_sb = sb("z_sb", [P, 2, W])
        h_tok = sb("h_tok", [P, GROUPS * W])
        a_in = sb("a_in", [P, GROUPS * W])
        state = sb("state", [P, KH, STEPS + 1, P])

        def h2_rows(g):
            return state[:, 0, bass.ds(G * g + 1, G), :]

        def z2_cols(g):
            return y_sb[:, bass.ds(g * W, W)]

        h_feat = sb("h_feat", [P, W])
        z_feat = sb("z_feat", [P, 2, W])
        logit_f = sb("logit_f", [P, P])
        g_in = sb("g_in", [P, G, E + 1])
        g_exp = sb("g_exp", [P, G, E + 1])
        g_max = sb("g_max", [P, G])
        g_den = sb("g_den", [P, 2, G])
        g_inv = sb("g_inv", [P, 2, G])
        g_p = sb("g_p", [P, G, E])
        g_w = sb("g_w", [P, G, E])
        g_wr = sb("g_wr", [P, G, E])
        g_sum = sb("g_sum", [P, G])
        g_sum1 = sb("g_sum1", [P, G])
        g_ws = sb("g_ws", [P, G])
        w_wide = sb("w_wide", [P, G, E, ER])
        w_feat = sb("w_feat", [P, W])
        hidden = sb("hidden", [P, 2, E, W])
        low = sb("low", [P, W])
        o_sb = sb("o_sb", [P, 2, W])

        diff = sb("diff", [P, KH, P])
        agree = sb("agree", [P, 1])
        cmp_col = sb("cmp_col", [P, 4])
        ok_row = sb("ok_row", [1, P])
        ok_f = sb("ok_f", [1, 1])
        ok_i = sb("ok_i", [1, 1], I32)

        bank = [ctx.enter_context(nc.psum_tensor(f"bank{i}", [P, W], F32)) for i in range(8)]

        names = """ident_zero ident_made x_landed x_landed2 tok_landed vec_landed rnn_landed ffn_landed
            zeroed x_zeroed vec_zeroed prep_done prep_copied adapt_done
            piece_ready patch_done patch_copied y_done y_ready bn_stats_done bn_step bn_pool
            hb_ready h_done h_stats h_kept ln_mv_ready ln_step z_ready z_done a_ready
            pre0 pre1 state0 state1
            diff_done diff_turned cmp_step cmp_turned ok_ready redo_pre redo_state
            wout_done hf_ready h2_done h2_ready h2_stats mv2_ready ln2_step z2_ready z2_done zf_ready
            zc_ready gate_done logit_ready logit_turned gate_step gate_sum exp_ready w_ready w_turned
            wf_ready fc1_done hidden_act hidden_dve low_done low_ready mix_done out_ready
            stored0 stored1 stored_cut"""
        S = {n: sem(n) for n in names.split()}

        def wait_past(eng, name, value):
            if not (isinstance(value, int) and value <= 0):
                eng.wait_ge(S[name], value)

        def wait_apart(eng, name, value):
            if not (isinstance(value, int) and value <= 0):
                eng.wait_ge(S[name], value)
                eng.nop(nofuse=True)

        def by_step(ap):
            return ap.rearrange("p (j c) -> p j c", j=G)

        def group_of(u):
            return (u + FIRST) % GROUPS

        def one(j):
            return slice(j * P, (j + 1) * P)

        rb = [[bank[0], bank[1]], [bank[2], bank[3]]]
        h_bank, z_bank = bank[4:6], bank[6:8]
        wo_bank, h2_bank, z2_bank = bank[4], bank[5], bank[6]
        fc_bank, gate_bank, w_bank, low_bank, mix_bank = bank[0:2], bank[2], bank[3], bank[7], bank[4]
        cmp_bank = bank[3]

        prep = [
            (0, [(tokw_raw[:, :], P, PATCH), (tokb_raw[:, :], 1, P)], [("tok_landed", 2)]),
            (0, [(wih_raw[:, m, :], P, P) for m in range(KH)] + [(vec_raw[:, :], 8, P)],
             [("rnn_landed", 2), ("vec_landed", 5)]),
            (1, [(whh_raw[:, m, k * P:(k + 1) * P], P, P) for m in range(KH) for k in range(KH)], []),
            (2, [(wout_raw[:, k * P:(k + 1) * P], P, P) for k in range(KH)]
             + [(gate_raw[:, :], ER, P), (lorab_raw[:, :], E * R, P)], [("ffn_landed", 7)]),
            (3, [(fc1_raw[:, e, :], P, P) for e in range(E)], []),
            (6, [(fc2_raw[:, e, :], P, P) for e in range(E)], []),
        ]
        PREP_TOK, PREP_IH, PREP_HH, PREP_OUT, PREP_FC1, PREP_FC2 = range(1, len(prep) + 1)

        block = ctx.enter_context(nc.Block())

        @block.sync
        def _(sp):
            rows = STEPS + CONTEXT - 1
            early = (2 * G + CONTEXT - 1) * D

            def x_rows(a, b):
                sp.dma_start(x_sb[0:COLS, a:b], bass.AP(tensor=x.tensor, offset=a,
                             ap=[[STEPS * D, CHUNKS - 1], [T * D, B], [1, b - a]]))\
                    .then_inc(S["x_landed" if a == 0 else "x_landed2"], 16)

            sp.dma_start(tokw_raw[:, :], tok_w).then_inc(S["tok_landed"], 16)
            x_rows(0, early)
            sp.wait_ge(S["x_zeroed"], 1)
            sp.dma_start(x_sb[COLS:P, 0:(LAST + CONTEXT - 1) * D],
                         bass.AP(tensor=x.tensor, offset=(CHUNKS - 1) * STEPS * D,
                                 ap=[[T * D, B], [1, (LAST + CONTEXT - 1) * D]])).then_inc(S["x_landed"], 16)
            x_rows(early, rows * D)
            sp.wait_ge(S["vec_zeroed"], 1)
            for r, v in ((0, tok_gamma), (1, tok_beta), (2, b_out)):
                sp.dma_start(vec_raw[r:r + 1, :], v.rearrange("(a d) -> a d", a=1)).then_inc(S["vec_landed"], 16)
            sp.dma_start(fc1_raw[:, :, :], fc1_w.rearrange("e h i -> h e i")).then_inc(S["ffn_landed"], 16)
            sp.dma_start(fc2_raw[:, :, :], fc2_w.rearrange("e d o -> d e o")).then_inc(S["ffn_landed"], 16)
            sp.wait_ge(S["zeroed"], 1)
            sp.dma_start(lora_a_sb[:, :, 0:R], lora_a.rearrange("e h r -> h e r")).then_inc(S["ffn_landed"], 16)
            sp.dma_start(lorab_raw[:, :], lora_b.rearrange("e r o -> (e r) o")).then_inc(S["ffn_landed"], 16)

            def store(c0, n_chunks, g, half, steps, name):
                sp.dma_start(
                    bass.AP(tensor=out.tensor, offset=(c0 * STEPS + G * g) * P,
                            ap=[[STEPS * P, n_chunks], [L * P, B], [1, steps * P]]),
                    o_sb[c0 * B:(c0 + n_chunks) * B, half, 0:steps * P]).then_inc(S[name], 16)

            def store_all(n0):
                with sp.Fori(0, FULL // 2) as p:
                    for half in range(2):
                        sp.wait_ge(S["out_ready"], n0 + 2 * p + half + 1)
                        store(0, CHUNKS, 2 * p + half, half, G, f"stored{half}")
                sp.wait_ge(S["out_ready"], n0 + FULL + 1)
                store(CHUNKS - 1, 1, FULL, 0, CUT, "stored_cut")
                sp.wait_ge(S["stored_cut"], 16 * (n0 // GROUPS + 1))
                store(0, CHUNKS - 1, FULL, 0, G, "stored0")
                sp.wait_ge(S["out_ready"], n0 + FULL + 2)
                store(0, CHUNKS - 1, FULL + 1, 1, G, "stored1")
                with sp.Fori(FULL // 2 + 1, GROUPS // 2) as p:
                    for half in range(2):
                        sp.wait_ge(S["out_ready"], n0 + 2 * p + half + 1)
                        store(0, CHUNKS - 1, 2 * p + half, half, G, f"stored{half}")
                for half in range(2):
                    sp.wait_ge(S[f"stored{half}"], 16 * (n0 + GROUPS) // 2)

            store_all(0)
            sp.wait_ge(S["ok_ready"], 1)
            ok = sp.value_load(ok_i[0:1, 0:1], min_val=0, max_val=1)
            with sp.If(ok == 0):
                store_all(GROUPS)
            sp.end_ifs()

        @block.gpsimd
        def _(pool):
            nc.gpsimd.memset(ident[:, :], 0.0).then_inc(S["ident_zero"], 1)
            pool.wait_ge(S["ident_zero"], 1)
            nc.gpsimd.affine_select(out=ident[:, :], in_=ident[:, :], compare_op=ALU.not_equal, fill=1.0,
                                    base=0, pattern=[[-1, P]], channel_multiplier=1).then_inc(S["ident_made"], 1)
            nc.gpsimd.memset(half_neg[:, :], -0.5)
            pool.wait_ge(S["x_landed"], 32)

            def piece(g, half):
                nc.gpsimd.tensor_copy(x_piece[:, half, :], x_sb[:, bass.ds(g * (G * D), XW)])\
                    .then_inc(S["piece_ready"], 1)

            piece(0, 0)
            piece(1, 1)
            pool.wait_ge(S["x_landed2"], 16)
            with pool.Fori(1, GROUPS // 2) as p:
                for half in range(2):
                    pool.wait_ge(S["patch_done"], 2 * p + (half - 1))
                    piece(2 * p + half, half)

            pool.wait_ge(S["bn_step"], 1)
            nc.gpsimd.tensor_scalar(bn_tmp[:, 0:1], bn_mv[:, 1:2], EPS, None, ALU.add).then_inc(S["bn_pool"], 1)
            pool.wait_ge(S["bn_pool"], 1)
            nc.gpsimd.tensor_tensor(bn_tmp[:, 1:2], bn_tmp[:, 0:1], half_neg[:, 0:1], ALU.pow)\
                .then_inc(S["bn_pool"], 1)

            def inverse_std(half, ready, n, step):
                wait_apart(pool, ready, n + 1)
                nc.gpsimd.tensor_scalar(ln_ve[:, half, :], ln_mv[:, half, :, 1], EPS, None, ALU.add)\
                    .then_inc(S[step], 1)
                pool.wait_ge(S[step], 2 * n + 1)
                nc.gpsimd.tensor_tensor(ln_rs[:, half, :], ln_ve[:, half, :], half_neg[:, :], ALU.pow)\
                    .then_inc(S[step], 1)

            with pool.Fori(0, GROUPS // 2) as p:
                for half in range(2):
                    inverse_std(half, "ln_mv_ready", 2 * p + half, "ln_step")

            def z_copy(g, half, n):
                pool.wait_ge(S["zf_ready"], n + 1)
                wait_apart(pool, "fc1_done", E * (n - 1))
                nc.gpsimd.tensor_copy(z_feat[:, half, :], z2_cols(g)).then_inc(S["zc_ready"], 1)

            def experts(n0):
                with pool.Fori(1, GROUPS // 2) as p:
                    for half in range(2):
                        z_copy(2 * p + half, half, n0 + 2 * p + half)

            with pool.Fori(0, GROUPS - 3) as q:
                inverse_std(0, "mv2_ready", q, "ln2_step")
            z_copy(0, 0, 0)
            inverse_std(0, "mv2_ready", GROUPS - 3, "ln2_step")
            z_copy(1, 1, 1)
            inverse_std(0, "mv2_ready", GROUPS - 2, "ln2_step")
            inverse_std(0, "mv2_ready", GROUPS - 1, "ln2_step")
            experts(0)
            pool.wait_ge(S["ok_ready"], 1)
            ok = pool.value_load(ok_i[0:1, 0:1], min_val=0, max_val=1)
            with pool.If(ok == 0):
                with pool.Fori(0, GROUPS) as q:
                    inverse_std(0, "mv2_ready", GROUPS + q, "ln2_step")
                z_copy(0, 0, GROUPS)
                z_copy(1, 1, GROUPS + 1)
                experts(GROUPS)
            pool.end_ifs()

        @block.scalar
        def _(act):
            act.dma_start(tokb_raw[:, :], tok_b.rearrange("(a d) -> a d", a=1)).then_inc(S["tok_landed"], 16)
            act.dma_start(wih_raw[:, :, :], w_ih.rearrange("(m h) i -> h m i", m=KH)).then_inc(S["rnn_landed"], 16)
            act.dma_start(whh_raw[:, :, :], w_hh.rearrange("(m h) i -> h m i", m=KH)).then_inc(S["rnn_landed"], 16)
            act.wait_ge(S["vec_zeroed"], 1)
            for r, v in ((4, b_ih), (6, b_hh)):
                act.dma_start(vec_raw[r:r + 2, :], v.rearrange("(m h) -> m h", m=KH))\
                    .then_inc(S["vec_landed"], 16)
            act.dma_start(wout_raw[:, :], w_out).then_inc(S["ffn_landed"], 16)
            act.wait_ge(S["zeroed"], 1)
            act.dma_start(gate_raw[0:E, :], gate_w).then_inc(S["ffn_landed"], 16)
            act.dma_start(gate_raw[E:E + 1, :], thr_w).then_inc(S["ffn_landed"], 16)

            def copied(dst, src):
                return nc.scalar.activation(dst, src, ACT.Copy)

            act.wait_ge(S["prep_done"], PREP_TOK)
            copied(tokw_t[:, :], bank[0][0:PATCH, 0:P])
            copied(tok_bias[:, :], bank[0][:, P:P + 1]).then_inc(S["prep_copied"], 1)

            act.wait_ge(S["prep_copied"], PREP_TOK)
            with act.Fori(0, GROUPS // 2) as p:
                for half in range(2):
                    act.wait_ge(S["y_done"], 2 * p + half + 1)
                    nc.scalar.activation(y_sb[:, bass.ds((2 * p + half) * W, W)], bank[6 + half][:, :],
                                         ACT.Relu, bias=tok_bias[:, 0:1]).then_inc(S["y_ready"], 1)

            act.wait_ge(S["prep_done"], PREP_IH)
            copied(vecs[:, :], bank[0][:, KH * P:KH * P + 8])
            copied(wih_t[:, :], bank[0][:, 0:KH * P]).then_inc(S["prep_copied"], 1)

            def bn_apply(u, half):
                if not (isinstance(u, int) and u < 2):
                    act.wait_ge(S["h_done"], u - 1)
                nc.scalar.activation(hb[:, half, :], y_sb[:, bass.ds(group_of(u) * W, W)], ACT.Identity,
                                     bias=bn_ab[:, 2:3], scale=bn_ab[:, 0:1]).then_inc(S["hb_ready"], 1)

            def keep_rows(u, half):
                act.wait_ge(S["h_stats"], u + 1)
                copied(h_tok[:, bass.ds(group_of(u) * W, W)], h_bank[half][:, :]).then_inc(S["h_kept"], 1)

            def keep_normed(u, half):
                act.wait_ge(S["z_done"], u + 1)
                copied(a_in[:, bass.ds(group_of(u) * W, W)], z_bank[half][:, :]).then_inc(S["a_ready"], 1)

            act.wait_ge(S["bn_step"], 4)
            bn_apply(0, 0)
            bn_apply(1, 1)
            act.wait_ge(S["prep_done"], PREP_HH)
            copied(whh_t[:, :], bank[1][:, :]).then_inc(S["prep_copied"], 1)
            keep_rows(0, 0)
            bn_apply(2, 0)
            keep_rows(1, 1)
            act.wait_ge(S["prep_done"], PREP_OUT)
            copied(wout_t[:, :], bank[2][:, 0:KH * P])
            copied(gate_t[:, :], bank[2][:, 2 * P:2 * P + ER])
            copied(lorab_t[:, :, 0:R], bank[2][:, 3 * P:3 * P + E * R].rearrange("p (e r) -> p e r", e=E))\
                .then_inc(S["prep_copied"], 1)
            act.wait_ge(S["prep_done"], PREP_FC1)
            copied(fc1_t[:, :], bank[3][:, :]).then_inc(S["prep_copied"], 1)
            act.wait_ge(S["prep_done"], PREP_FC2)
            copied(fc2_t[:, :], bank[6][:, :]).then_inc(S["prep_copied"], 1)
            act.wait_ge(S["prep_done"], len(prep) + 1)
            copied(adapt[:, :], bank[7][:, 0:P]).then_inc(S["adapt_done"], 1)

            def relu1(n, slot, a, parity, cols):
                act.wait_ge(S["pre1"], n + 1)
                nc.scalar.activation(state[:, 1, slot, a:a + cols], rb[1][parity][:, 0:cols], ACT.Relu,
                                     bias=bias_h[:, 1:2]).then_inc(S["state1"], 1)

            def warm(i, more):
                a, b = 2 * i + 2, 2 * i + 3
                keep_normed(a - 2, 0)
                relu1(G * i, 1, B, 0, COLS)
                bn_apply(b, 1)
                relu1(G * i + 1, 0, B, 1, COLS)
                keep_rows(a, 0)
                if more:
                    bn_apply(a + 2, 0)
                relu1(G * i + 2, 1, B, 0, COLS)
                keep_normed(b - 2, 1)
                keep_rows(b, 1)
                relu1(G * i + 3, 0, B, 1, COLS)

            with act.Fori(0, WARM // G - 1) as i:
                warm(i, True)
            warm(WARM // G - 1, False)

            def attn_out(n):
                act.wait_ge(S["wout_done"], n + 1)
                wait_past(act, "h2_done", n)
                nc.scalar.activation(h_feat[:, :], wo_bank[:, :], ACT.Identity, bias=vecs[:, 2:3])\
                    .then_inc(S["hf_ready"], 1)

            def keep_z2(q, n):
                act.wait_ge(S["z2_done"], n + 1)
                copied(z2_cols(q), z2_bank[:, :]).then_inc(S["zf_ready"], 1)

            def main(g):
                first = isinstance(g, int)
                for j in range(G):
                    if j == 0:
                        if first and g == 0:
                            keep_normed(GROUPS - 2, 0)
                        if not first or g >= 3:
                            keep_z2(g - 3, g - 3)
                    if j == 2:
                        if first and g == 0:
                            keep_normed(GROUPS - 1, 1)
                        if not first or g >= 1:
                            attn_out(g - 1)
                    relu1(WARM + G * g + j, bass.ds(G * g + j + 1, 1), 0, j % 2, P)

            for g in range(3):
                main(g)
            with act.Fori(3, GROUPS) as g:
                main(g)
            keep_z2(GROUPS - 3, GROUPS - 3)

            def logits(n):
                act.wait_ge(S["gate_done"], n + 1)
                wait_past(act, "logit_turned", n)
                copied(logit_f[:, :], gate_bank[:, 0:P]).then_inc(S["logit_ready"], 1)

            def unit(n, e, half):
                act.wait_ge(S["fc1_done"], E * n + e + 1)
                wait_past(act, "low_done", n - 1)
                nc.scalar.activation(hidden[:, half, e, :], fc_bank[e % 2][:, :], ACT.Relu)\
                    .then_inc(S["hidden_act"], 1)

            def spread_w(n):
                act.wait_ge(S["w_turned"], n + 1)
                wait_past(act, "low_ready", n)
                copied(w_feat[:, :], w_bank[:, :]).then_inc(S["wf_ready"], 1)

            def group(n, half, more, before=True, a=None, b=None):
                unit(n, 0, half)
                if a:
                    a()
                if before:
                    spread_w(n - 1)
                act.wait_ge(S["gate_step"], 10 * n + 3)
                nc.scalar.activation(g_exp[:, :, :], g_in[:, :, :], ACT.Exp).then_inc(S["exp_ready"], 1)
                unit(n, 2, half)
                act.wait_ge(S["gate_step"], 10 * n + 10)
                wait_past(act, "w_turned", n)
                for j in range(G):
                    last = nc.scalar.activation(
                        w_wide[:, j, :, :], g_wr[:, j, :].unsqueeze(2).to_broadcast([P, E, ER]),
                        ACT.Copy, scale=g_ws[:, j:j + 1])
                last.then_inc(S["w_ready"], 1)
                if b:
                    b()
                if more:
                    logits(n + 1)

            def experts(n0, hooks):
                logits(n0)
                group(n0, 0, True, before=False, **hooks.get(0, {}))
                group(n0 + 1, 1, True, **hooks.get(1, {}))
                with act.Fori(1, GROUPS // 2 - 1) as p:
                    for half in range(2):
                        group(n0 + 2 * p + half, half, True)
                group(n0 + GROUPS - 2, 0, True)
                group(n0 + GROUPS - 1, 1, False)
                spread_w(n0 + GROUPS - 1)

            experts(0, {0: {"a": lambda: attn_out(GROUPS - 1),
                            "b": lambda: keep_z2(GROUPS - 2, GROUPS - 2)},
                        1: {"b": lambda: keep_z2(GROUPS - 1, GROUPS - 1)}})
            act.wait_ge(S["ok_ready"], 1)
            ok = act.value_load(ok_i[0:1, 0:1], min_val=0, max_val=1)
            with act.If(ok == 0):
                with act.Fori(0, GROUPS) as q:
                    attn_out(GROUPS + q)
                    keep_z2(q, GROUPS + q)
                experts(GROUPS, {})
            act.end_ifs()

        @block.vector
        def _(dve):
            nc.vector.memset(vec_raw[:, :], 0.0).then_inc(S["vec_zeroed"], 1)
            nc.vector.memset(x_sb[96:P, (LAST + CONTEXT - 1) * D:], 0.0).then_inc(S["x_zeroed"], 1)
            nc.vector.memset(gate_raw[:, :], 0.0)
            nc.vector.memset(lora_a_sb[:, :, :], 0.0)
            nc.vector.memset(lorab_t[:, :, :], 0.0).then_inc(S["zeroed"], 1)
            for k in range(KH):
                nc.vector.memset(state[:, k, 0:2, :], 0.0).then_inc(S[f"state{k}"], 1)

            def patch_copy(g, half):
                dve.wait_ge(S["patch_done"], g + 1)
                wait_past(dve, "y_done", g - 1)
                nc.vector.tensor_copy(patch_t[:, half, :], bank[4 + half][0:PATCH, :])\
                    .then_inc(S["patch_copied"], 1)

            def stats(g):
                wait_apart(dve, "y_ready", g + 1)
                nc.vector.bn_stats(bn_st[:, bass.ds(g, 1), :], y_sb[:, bass.ds(g * W, W)])\
                    .then_inc(S["bn_stats_done"], 1)

            def stats_short(g):
                wait_apart(dve, "y_ready", g + 1)
                nc.vector.bn_stats(bn_st[:, g, :], by_step(y_sb[:, g * W:(g + 1) * W])[:, :, 0:COLS])\
                    .then_inc(S["bn_stats_done"], 1)

            def stats_cut(g):
                dve.wait_ge(S["y_ready"], g + 1)
                nc.vector.bn_stats(bn_st[:, g, :], y_sb[:, g * W:g * W + CUT * P])
                nc.vector.bn_stats(bn_st[:, GROUPS, :], by_step(y_sb[:, g * W:(g + 1) * W])[:, CUT:G, 0:COLS])\
                    .then_inc(S["bn_stats_done"], 1)

            patch_copy(0, 0)
            patch_copy(1, 1)
            with dve.Fori(1, FULL // 2 + 1) as p:
                for half in range(2):
                    patch_copy(2 * p + half, half)
                    stats(2 * p + half - 2)
            for g in range(FULL + 2, GROUPS + 2):
                if g < GROUPS:
                    patch_copy(g, g % 2)
                (stats_cut if g - 2 == FULL else stats_short)(g - 2)

            dve.wait_ge(S["bn_stats_done"], GROUPS)
            nc.vector.bn_aggr(bn_mv[:, :], bn_st[:, :, :]).then_inc(S["bn_step"], 1)
            dve.wait_ge(S["prep_copied"], PREP_IH)
            nc.vector.tensor_tensor(bias_h[:, :], vecs[:, 4:6], vecs[:, 6:8], ALU.add)
            dve.wait_ge(S["bn_pool"], 2)
            nc.vector.tensor_tensor(bn_ab[:, 0:1], vecs[:, 0:1], bn_tmp[:, 1:2], ALU.mult).then_inc(S["bn_step"], 1)
            dve.wait_ge(S["bn_step"], 2)
            nc.vector.tensor_tensor(bn_ab[:, 1:2], bn_mv[:, 0:1], bn_ab[:, 0:1], ALU.mult).then_inc(S["bn_step"], 1)
            dve.wait_ge(S["bn_step"], 3)
            nc.vector.tensor_tensor(bn_ab[:, 2:3], vecs[:, 1:2], bn_ab[:, 1:2], ALU.subtract)\
                .then_inc(S["bn_step"], 1)

            def ln1_stats(u, half):
                wait_apart(dve, "h_done", u + 1)
                for j in range(G):
                    last = nc.vector.bn_stats(ln_st[:, half, j, :], h_bank[half][:, one(j)])
                last.then_inc(S["h_stats"], 1)

            def ln1_moments(u, half):
                wait_apart(dve, "h_stats", u + 1)
                for j in range(G):
                    last = nc.vector.bn_aggr(ln_mv[:, half, j, :], ln_st[:, half, j, :])
                last.then_inc(S["ln_mv_ready"], 1)

            def ln1_norm(u, half):
                dve.wait_ge(S["ln_step"], 2 * u + 2)
                dve.wait_ge(S["h_kept"], u + 1)
                wait_past(dve, "z_done", u - 1)
                for j in range(G):
                    last = nc.vector.tensor_scalar(
                        z_sb[:, half, one(j)], h_tok[:, bass.ds(group_of(u) * W + j * P, P)],
                        ln_mv[:, half, j, 0:1], ln_rs[:, half, j:j + 1], ALU.subtract, ALU.mult)
                last.then_inc(S["z_ready"], 1)

            def relu0(n, slot, a, parity, cols):
                dve.wait_ge(S["pre0"], n + 1)
                nc.vector.tensor_scalar(state[:, 0, slot, a:a + cols], rb[0][parity][:, 0:cols],
                                        bias_h[:, 0:1], 0.0, ALU.add, ALU.max).then_inc(S["state0"], 1)

            ln1_stats(0, 0)
            ln1_moments(0, 0)
            ln1_stats(1, 1)
            ln1_moments(1, 1)
            ln1_norm(0, 0)
            ln1_norm(1, 1)
            with dve.Fori(0, WARM // G) as i:
                a, b = 2 * i + 2, 2 * i + 3
                relu0(G * i, 1, B, 0, COLS)
                ln1_stats(a, 0)
                relu0(G * i + 1, 0, B, 1, COLS)
                ln1_moments(a, 0)
                ln1_stats(b, 1)
                relu0(G * i + 2, 1, B, 0, COLS)
                ln1_moments(b, 1)
                ln1_norm(a, 0)
                relu0(G * i + 3, 0, B, 1, COLS)
                ln1_norm(b, 1)

            def h2(q, n):
                dve.wait_ge(S["h2_done"], n + 1)
                nc.vector.tensor_tensor(h2_rows(q), by_step(h2_bank[:, :]), by_step(h_tok[:, bass.ds(q * W, W)]),
                                        ALU.add).then_inc(S["h2_ready"], 1)

            def h2_stats(q, n):
                wait_apart(dve, "h2_ready", n + 1)
                for j in range(G):
                    last = nc.vector.bn_stats(ln_st[:, 0, j, :], state[:, 0, bass.ds(G * q + j + 1, 1), :])
                last.then_inc(S["h2_stats"], 1)

            def h2_moments(n):
                wait_apart(dve, "h2_stats", n + 1)
                for j in range(G):
                    last = nc.vector.bn_aggr(ln_mv[:, 0, j, :], ln_st[:, 0, j, :])
                last.then_inc(S["mv2_ready"], 1)

            def h2_norm(q, n):
                dve.wait_ge(S["ln2_step"], 2 * n + 2)
                wait_past(dve, "z2_done", n)
                for j in range(G):
                    last = nc.vector.tensor_scalar(
                        z_sb[:, 0, one(j)], state[:, 0, bass.ds(G * q + j + 1, 1), :],
                        ln_mv[:, 0, j, 0:1], ln_rs[:, 0, j:j + 1], ALU.subtract, ALU.mult)
                last.then_inc(S["z2_ready"], 1)

            def main(g):
                first = isinstance(g, int)
                for j in range(G):
                    relu0(WARM + G * g + j, bass.ds(G * g + j + 1, 1), 0, j % 2, P)
                    if j == 3 and (not first or g >= 1):
                        h2(g - 1, g - 1)
                    if not first or g >= 2:
                        if j == 0:
                            h2_stats(g - 2, g - 2)
                        if j == 1:
                            h2_moments(g - 2)
                        if j == 2:
                            h2_norm(g - 2, g - 2)

            for g in range(2):
                main(g)
            with dve.Fori(2, GROUPS) as g:
                main(g)

            dve.wait_ge(S["state0"], WARM + STEPS + 1)
            dve.wait_ge(S["state1"], WARM + STEPS + 1)
            nc.vector.tensor_tensor(diff[:, :, 0:COLS], state[:, :, 0, B:P], state[:, :, STEPS, 0:COLS],
                                    ALU.subtract).then_inc(S["diff_done"], 1)
            h2_stats(GROUPS - 2, GROUPS - 2)
            h2_moments(GROUPS - 2)
            dve.wait_ge(S["diff_turned"], 1)
            turned = cmp_bank[0:COLS, :].rearrange("p (a c) -> p a c", a=2)
            nc.vector.tensor_reduce(cmp_col[0:COLS, 0:2], turned, AX_X, ALU.max)
            nc.vector.tensor_reduce(cmp_col[0:COLS, 2:3], turned[:, 0, :], AX_X, ALU.min)\
                .then_inc(S["cmp_step"], 1)
            h2_norm(GROUPS - 2, GROUPS - 2)
            dve.wait_ge(S["cmp_step"], 1)
            nc.vector.scalar_tensor_tensor(cmp_col[0:COLS, 3:4], cmp_col[0:COLS, 2:3], -1.0,
                                           cmp_col[0:COLS, 0:1], ALU.mult, ALU.max).then_inc(S["cmp_step"], 1)
            dve.wait_ge(S["cmp_step"], 2)
            nc.vector.scalar_tensor_tensor(agree[0:COLS, :], cmp_col[0:COLS, 1:2], TOL,
                                           cmp_col[0:COLS, 3:4], ALU.mult, ALU.is_ge).then_inc(S["cmp_step"], 1)

            def verdict():
                dve.wait_ge(S["cmp_turned"], 1)
                nc.vector.tensor_reduce(ok_f[:, :], cmp_bank[0:1, 0:COLS], AX_X, ALU.min)\
                    .then_inc(S["cmp_step"], 1)
                dve.wait_ge(S["cmp_step"], 4)
                nc.vector.tensor_copy(ok_i[:, :], ok_f[:, :]).then_inc(S["ok_ready"], 1)

            def over_experts(v, n):
                return v.unsqueeze(2).to_broadcast([P, G, n])

            def gates_a(n):
                dve.wait_ge(S["logit_turned"], n + 1)
                lg = gate_bank[:, P:2 * P].rearrange("p (j c) -> p j c", j=G)
                nc.vector.tensor_reduce(g_max[:, :], lg[:, :, 0:E], AX_X, ALU.max).then_inc(S["gate_step"], 1)
                nc.vector.tensor_scalar(g_in[:, :, E], lg[:, :, E], -1.0, None, ALU.mult).then_inc(S["gate_step"], 1)
                dve.wait_ge(S["gate_step"], 10 * n + 1)
                nc.vector.tensor_tensor(g_in[:, :, 0:E], lg[:, :, 0:E], over_experts(g_max[:, :], E),
                                        ALU.subtract).then_inc(S["gate_step"], 1)

            def gates_b(n):
                def step(k, instr):
                    instr.then_inc(S["gate_step"], 1)
                    dve.wait_ge(S["gate_step"], 10 * n + k)

                dve.wait_ge(S["exp_ready"], n + 1)
                nc.vector.tensor_reduce(g_den[:, 0, :], g_exp[:, :, 0:E], AX_X, ALU.add)
                step(4, nc.vector.tensor_scalar(g_den[:, 1, :], g_exp[:, :, E], float(E), float(E),
                                                ALU.mult, ALU.add))
                step(5, nc.vector.reciprocal(g_inv[:, :, :], g_den[:, :, :]))
                step(6, nc.vector.tensor_tensor(g_p[:, :, :], g_exp[:, :, 0:E],
                                                over_experts(g_inv[:, 0, :], E), ALU.mult))
                step(7, nc.vector.tensor_tensor(g_w[:, :, :], g_p[:, :, :],
                                                over_experts(g_inv[:, 1, :], E), ALU.subtract))
                step(8, nc.vector.tensor_scalar(g_wr[:, :, :], g_w[:, :, :], 0.0, None, ALU.max))
                step(9, nc.vector.tensor_reduce(g_sum[:, :], g_wr[:, :, :], AX_X, ALU.add))
                nc.vector.scalar_tensor_tensor(g_sum1[:, :], g_sum[:, :], 0.0, g_sum[:, :],
                                               ALU.is_equal, ALU.add).then_inc(S["gate_sum"], 1)
                dve.wait_ge(S["gate_sum"], n + 1)
                nc.vector.reciprocal(g_ws[:, :], g_sum1[:, :]).then_inc(S["gate_step"], 1)

            def unit(n, e, half):
                dve.wait_ge(S["fc1_done"], E * n + e + 1)
                wait_past(dve, "low_done", n - 1)
                nc.vector.tensor_scalar(hidden[:, half, e, :], fc_bank[e % 2][:, :], 0.0, None, ALU.max)\
                    .then_inc(S["hidden_dve"], 1)

            def weigh(n):
                dve.wait_ge(S["wf_ready"], n + 1)
                dve.wait_ge(S["low_done"], n + 1)
                wait_past(dve, "mix_done", n)
                nc.vector.tensor_tensor(low[:, :], low_bank[:, :], w_feat[:, :], ALU.mult).then_inc(S["low_ready"], 1)

            def add_up(g, n, half, earlier):
                dve.wait_ge(S["mix_done"], n + 1)
                wait_past(dve, f"stored{half}", 16 * earlier)
                nc.vector.tensor_tensor(by_step(o_sb[:, half, :]), by_step(mix_bank[:, :]), h2_rows(g), ALU.add)\
                    .then_inc(S["out_ready"], 1)

            def group(g, n, half, pair, before=True, a=None, b=None):
                gates_a(n)
                if before:
                    weigh(n - 1)
                unit(n, 1, half)
                if a:
                    a()
                gates_b(n)
                if b:
                    b()
                unit(n, 3, half)
                if before:
                    add_up(g - 1, n - 1, 1 - half, pair - (1 - half))

            def experts(n0, hooks):
                m0 = n0 // 2
                group(0, n0, 0, m0, before=False, **hooks.get(0, {}))
                group(1, n0 + 1, 1, m0, **hooks.get(1, {}))
                for half in range(2):
                    group(2 + half, n0 + 2 + half, half, m0 + 1)
                with dve.Fori(2, GROUPS // 2) as p:
                    for half in range(2):
                        group(2 * p + half, n0 + 2 * p + half, half, m0 + p)
                weigh(n0 + GROUPS - 1)
                add_up(GROUPS - 1, n0 + GROUPS - 1, 1, m0 + GROUPS // 2 - 1)

            def last_stats():
                h2_stats(GROUPS - 1, GROUPS - 1)
                h2_moments(GROUPS - 1)
                verdict()

            experts(0, {0: {"a": lambda: h2(GROUPS - 1, GROUPS - 1), "b": last_stats},
                        1: {"a": lambda: h2_norm(GROUPS - 1, GROUPS - 1)}})
            dve.wait_ge(S["ok_ready"], 1)
            ok = dve.value_load(ok_i[0:1, 0:1], min_val=0, max_val=1)
            with dve.If(ok == 0):
                def redo_step(n, s, col):
                    dve.wait_ge(S["redo_pre"], n + 1)
                    for m in range(KH):
                        last = nc.vector.tensor_scalar(
                            state[:, m, bass.ds(s + 1, 1), bass.ds(col, B)], bank[m][:, 0:B],
                            bias_h[:, m:m + 1], 0.0, ALU.add, ALU.max)
                    last.then_inc(S["redo_state"], 1)

                dve.wait_ge(S["out_ready"], GROUPS)
                nc.vector.memset(state[:, :, 0, 0:B], 0.0).then_inc(S["redo_state"], 1)
                with dve.Fori(0, CHUNKS - 1) as c:
                    with dve.Fori(0, STEPS) as s:
                        redo_step(c * STEPS + s, s, c * B)
                    dve.wait_ge(S["redo_state"], (c + 1) * (STEPS + 1))
                    nc.vector.tensor_copy(state[:, :, 0, bass.ds(c * B + B, B)],
                                          state[:, :, STEPS, bass.ds(c * B, B)]).then_inc(S["redo_state"], 1)
                with dve.Fori(0, STEPS) as s:
                    redo_step((CHUNKS - 1) * STEPS + s, s, COLS)
                with dve.Fori(0, GROUPS) as q:
                    h2(q, GROUPS + q)
                    h2_stats(q, GROUPS + q)
                    h2_moments(GROUPS + q)
                    h2_norm(q, GROUPS + q)
                experts(GROUPS, {})
            dve.end_ifs()

        @block.tensor
        def _(pe):
            def turn(n):
                b, sources, loads = prep[n - 1]
                for name, count in loads:
                    pe.wait_ge(S[name], 16 * count)
                for i, (src, rows, cols) in enumerate(sources):
                    last = nc.tensor.transpose(bank[b][0:cols, i * P:i * P + rows], src, ident[0:rows, 0:rows])
                last.then_inc(S["prep_done"], 1)

            pe.wait_ge(S["ident_made"], 1)
            turn(PREP_TOK)

            def patches(g, half):
                pe.wait_ge(S["piece_ready"], g + 1)
                wait_past(pe, "patch_copied", g - 1)
                for j in range(G):
                    last = nc.tensor.transpose(bank[4 + half][0:PATCH, one(j)],
                                               x_piece[:, half, j * D:j * D + PATCH], ident[:, :])
                last.then_inc(S["patch_done"], 1)

            def tdnn(g, half):
                pe.wait_ge(S["patch_copied"], g + 1)
                wait_past(pe, "y_ready", g - 1)
                nc.tensor.matmul(bank[6 + half][:, :], tokw_t[:, :], patch_t[:, half, :], start=True, stop=True)\
                    .then_inc(S["y_done"], 1)

            patches(0, 0)
            patches(1, 1)
            pe.wait_ge(S["prep_copied"], PREP_TOK)
            tdnn(0, 0)
            patches(2, 0)
            tdnn(1, 1)
            patches(3, 1)
            tdnn(2, 0)
            with pe.Fori(2, GROUPS // 2) as p:
                patches(2 * p, 0)
                tdnn(2 * p - 1, 1)
                patches(2 * p + 1, 1)
                tdnn(2 * p, 0)
            turn(PREP_IH)
            tdnn(GROUPS - 1, 1)
            turn(PREP_HH)
            turn(PREP_OUT)
            turn(PREP_FC1)
            pe.wait_ge(S["y_ready"], GROUPS)
            turn(PREP_FC2)

            def ln1_turn(u, half):
                pe.wait_ge(S["hb_ready"], u + 1)
                wait_past(pe, "h_kept", u - 1)
                for j in range(G):
                    last = nc.tensor.transpose(h_bank[half][:, one(j)], hb[:, half, one(j)], ident[:, :])
                last.then_inc(S["h_done"], 1)

            def ln1_back(u, half):
                pe.wait_ge(S["z_ready"], u + 1)
                wait_past(pe, "a_ready", u - 1)
                for j in range(G):
                    last = nc.tensor.transpose(z_bank[half][:, one(j)], z_sb[:, half, one(j)], ident[:, :])
                last.then_inc(S["z_done"], 1)

            pe.wait_ge(S["patch_copied"], GROUPS)
            ln1_turn(0, 0)
            ln1_turn(1, 1)
            ln1_turn(2, 0)
            pe.wait_ge(S["prep_copied"], PREP_FC2)
            for e in range(E):
                last = nc.tensor.matmul(bank[7][ER * e:ER * (e + 1), 0:P], lorab_t[:, e, :],
                                        fc2_t[:, one(e)], start=True, stop=True)
            last.then_inc(S["prep_done"], 1)
            ln1_back(0, 0)

            def project(parity, col, cols):
                for m in range(KH):
                    nc.tensor.matmul(rb[m][parity][:, 0:cols], wih_t[:, one(m)],
                                     a_in[:, bass.ds(col, cols)], start=True, stop=False)

            def recur(n, parity, rhs, cols):
                for k in range(KH):
                    pe.wait_ge(S["state0" if k == 0 else "state1"], n + 1)
                    for m in range(KH):
                        mm = nc.tensor.matmul(rb[m][parity][:, 0:cols], whh_t[:, one(m * KH + k)],
                                              rhs(k), start=False, stop=(k == KH - 1))
                        if k == KH - 1:
                            mm.then_inc(S["pre0" if m == 0 else "pre1"], 1)

            WARM_COL = (STEPS - WARM) * P
            pe.wait_ge(S["adapt_done"], 1)
            pe.wait_ge(S["a_ready"], 1)
            project(0, WARM_COL, COLS)

            def warm(i, more):
                a, b = 2 * i + 2, 2 * i + 3
                for j in range(G):
                    recur(G * i + j, j % 2, lambda k: state[:, k, j % 2, B:P], COLS)
                    if j < G - 1:
                        project((j + 1) % 2, WARM_COL + (G * i + j + 1) * P, COLS)
                    elif more:
                        pe.wait_ge(S["a_ready"], i + 2)
                        project(0, WARM_COL + (G * i + G) * P, COLS)
                    else:
                        project(0, 0, P)
                    if j == 0:
                        ln1_back(b - 2, 1)
                    elif j == 1:
                        ln1_turn(b, 1)
                    elif j == 2 and more:
                        ln1_turn(a + 2, 0)
                    elif j == 3:
                        ln1_back(a, 0)

            with pe.Fori(0, WARM // G - 1) as i:
                warm(i, True)
            warm(WARM // G - 1, False)

            def w_out(q, k, n):
                if k == 0:
                    wait_past(pe, "hf_ready", n)
                mm = nc.tensor.matmul(wo_bank[:, :], wout_t[:, one(k)], state[:, k, bass.ds(G * q + 1, G), :],
                                      start=(k == 0), stop=(k == KH - 1))
                if k == KH - 1:
                    mm.then_inc(S["wout_done"], 1)

            def h2_turn(n):
                pe.wait_ge(S["hf_ready"], n + 1)
                wait_past(pe, "h2_ready", n)
                for j in range(G):
                    last = nc.tensor.transpose(h2_bank[:, one(j)], h_feat[:, one(j)], ident[:, :])
                last.then_inc(S["h2_done"], 1)

            def z2_turn(n):
                pe.wait_ge(S["z2_ready"], n + 1)
                wait_past(pe, "zf_ready", n)
                for j in range(G):
                    last = nc.tensor.transpose(z2_bank[:, one(j)], z_sb[:, 0, one(j)], ident[:, :])
                last.then_inc(S["z2_done"], 1)

            def main(g, more):
                first = isinstance(g, int)
                for j in range(G):
                    recur(WARM + G * g + j, j % 2, lambda k: state[:, k, bass.ds(G * g + j, 1), :], P)
                    if j < G - 1 or more:
                        project((j + 1) % 2, (G * g + j + 1) * P, P)
                    if first and g == 0 and j == 1:
                        ln1_back(GROUPS - 1, 1)
                    if j == 3 and first and g == 0:
                        pe.wait_ge(S["a_ready"], GROUPS)
                    if j == 3 and (not first or g >= 2):
                        z2_turn(g - 2)
                    if not first or g >= 1:
                        if j < 2:
                            w_out(g - 1, j, g - 1)
                        elif j == 2:
                            h2_turn(g - 1)

            pe.wait_ge(S["h_kept"], GROUPS)
            for g in range(2):
                main(g, True)
            with pe.Fori(2, GROUPS - 1) as g:
                main(g, True)
            main(GROUPS - 1, False)

            def gate(n, half):
                pe.wait_ge(S["zc_ready"], n + 1)
                wait_past(pe, "gate_step", 10 * n - 7)
                for j in range(G):
                    last = nc.tensor.matmul(gate_bank[ER * j:ER * (j + 1), 0:P], gate_t[:, :],
                                            z_feat[:, half, one(j)], start=True, stop=True)
                last.then_inc(S["gate_done"], 1)

            def gate_turn(n):
                pe.wait_ge(S["logit_ready"], n + 1)
                nc.tensor.transpose(gate_bank[:, P:2 * P], logit_f[:, :], ident[:, :]).then_inc(S["logit_turned"], 1)

            def fc1(n, e, half):
                wait_past(pe, "hidden_act" if e % 2 == 0 else "hidden_dve", 2 * n + e // 2)
                nc.tensor.matmul(fc_bank[e % 2][:, :], fc1_t[:, one(e)], z_feat[:, half, :],
                                 start=True, stop=True).then_inc(S["fc1_done"], 1)

            def low_rank(n, half):
                pe.wait_ge(S["hidden_act"], 2 * n + 2)
                pe.wait_ge(S["hidden_dve"], 2 * n + 2)
                wait_past(pe, "low_ready", n)
                for e in range(E):
                    last = nc.tensor.matmul(low_bank[ER * e:ER * (e + 1), :], lora_a_sb[:, e, :],
                                            hidden[:, half, e, :], start=True, stop=True)
                last.then_inc(S["low_done"], 1)

            def w_turn(n):
                pe.wait_ge(S["w_ready"], n + 1)
                wait_past(pe, "wf_ready", n)
                if isinstance(n, int) and n == 0:
                    pe.wait_ge(S["cmp_step"], 4)
                for j in range(G):
                    last = nc.tensor.transpose(w_bank[:, one(j)], w_wide[:, j, :, :], ident[:, :])
                last.then_inc(S["w_turned"], 1)

            def mix(n):
                pe.wait_ge(S["low_ready"], n + 1)
                wait_past(pe, "out_ready", n)
                for j in range(G):
                    last = nc.tensor.matmul(mix_bank[:, one(j)], low[:, one(j)], adapt[:, :], start=True, stop=True)
                last.then_inc(S["mix_done"], 1)

            def group(n, half, more, before=True, a=None, b=None, c=None):
                fc1(n, 0, half)
                if before:
                    low_rank(n - 1, 1 - half)
                    w_turn(n - 1)
                if a:
                    a()
                gate_turn(n)
                fc1(n, 1, half)
                if b:
                    b()
                fc1(n, 2, half)
                if before:
                    mix(n - 1)
                if c:
                    c()
                fc1(n, 3, half)
                if more:
                    gate(n + 1, 1 - half)

            def experts(n0, hooks):
                gate(n0, 0)
                group(n0, 0, True, before=False, **hooks.get(0, {}))
                group(n0 + 1, 1, True, **hooks.get(1, {}))
                with pe.Fori(1, GROUPS // 2 - 1) as p:
                    for half in range(2):
                        group(n0 + 2 * p + half, half, True)
                group(n0 + GROUPS - 2, 0, True)
                group(n0 + GROUPS - 1, 1, False)
                low_rank(n0 + GROUPS - 1, 1)
                w_turn(n0 + GROUPS - 1)
                mix(n0 + GROUPS - 1)

            def compare():
                pe.wait_ge(S["diff_done"], 1)
                for k in range(KH):
                    nc.tensor.transpose(cmp_bank[0:COLS, one(k)], diff[:, k, 0:COLS], ident[:, :])
                    last = nc.tensor.transpose(cmp_bank[0:COLS, one(KH + k)], state[:, k, STEPS, 0:COLS],
                                               ident[:, :])
                last.then_inc(S["diff_turned"], 1)

            def finish_rnn():
                for k in range(KH):
                    w_out(GROUPS - 1, k, GROUPS - 1)

            def last_turn():
                h2_turn(GROUPS - 1)
                pe.wait_ge(S["cmp_step"], 3)
                nc.tensor.transpose(cmp_bank[0:1, 0:COLS], agree[0:COLS, :], ident[0:COLS, 0:COLS])\
                    .then_inc(S["cmp_turned"], 1)

            pe.wait_ge(S["state0"], WARM + STEPS + 1)
            pe.wait_ge(S["state1"], WARM + STEPS + 1)
            compare()
            experts(0, {0: {"a": finish_rnn, "b": lambda: z2_turn(GROUPS - 2), "c": last_turn},
                        1: {"c": lambda: z2_turn(GROUPS - 1)}})
            pe.wait_ge(S["ok_ready"], 1)
            ok = pe.value_load(ok_i[0:1, 0:1], min_val=0, max_val=1)
            with pe.If(ok == 0):
                def redo_step(n, s, col):
                    pe.wait_ge(S["redo_state"], n)
                    for m in range(KH):
                        nc.tensor.matmul(bank[m][:, 0:B], wih_t[:, one(m)],
                                         a_in[:, bass.ds(s * P + col, B)], start=True, stop=False)
                        for k in range(KH):
                            last = nc.tensor.matmul(
                                bank[m][:, 0:B], whh_t[:, one(m * KH + k)],
                                state[:, k, bass.ds(s, 1), bass.ds(col, B)], start=False, stop=(k == KH - 1))
                    last.then_inc(S["redo_pre"], 1)

                with pe.Fori(0, CHUNKS - 1) as c:
                    with pe.Fori(0, STEPS) as s:
                        redo_step(c * (STEPS + 1) + s + 1, s, c * B)
                with pe.Fori(0, STEPS) as s:
                    redo_step((CHUNKS - 1) * (STEPS + 1) + s + 1, s, COLS)
                pe.wait_ge(S["redo_state"], CHUNKS * (STEPS + 1))
                pe.wait_ge(S["out_ready"], GROUPS)
                with pe.Fori(0, GROUPS) as q:
                    for k in range(KH):
                        w_out(q, k, GROUPS + q)
                    h2_turn(GROUPS + q)
                    z2_turn(GROUPS + q)
                experts(GROUPS, {})
            pe.end_ifs()


_INS = ['x', 'L0_tok_W', 'L0_tok_b', 'L0_tok_gamma', 'L0_tok_beta', 'L0_attn_W_ih', 'L0_attn_W_hh',
        'L0_attn_b_ih', 'L0_attn_b_hh', 'L0_attn_W_out', 'L0_attn_b_out', 'L0_ffn_gate_w', 'L0_ffn_thr_w',
        'L0_ffn_fc1_w', 'L0_ffn_lora_A', 'L0_ffn_lora_B', 'L0_ffn_fc2_w']


def kernel(**inputs):
    import numpy as _np
    import concourse.bacc as _bacc
    from concourse import mybir as _mybir
    from concourse.bass_utils import run_bass_kernel_spmd as _run

    nc = _bacc.Bacc("TRN2", target_bir_lowering=False, num_devices=1)
    arrays, args = {}, []
    for name in _INS:
        a = _np.ascontiguousarray(inputs[name])
        arrays[f"in_{name}_dram"] = a
        args.append(nc.dram_tensor(f"in_{name}_dram", a.shape, _mybir.dt.from_np(a.dtype), kind="ExternalInput").ap())
    B, T, D = inputs['x'].shape
    O, F = inputs['L0_tok_W'].shape
    out = nc.dram_tensor("out_dram", (B, T - F // D + 1, O), _mybir.dt.float32, kind="ExternalOutput").ap()
    audio_tower(nc, *args, out)
    r = _run(nc, [arrays], core_ids=[0])
    return r.results[0]["out_dram"]
```

```python
from contextlib import ExitStack

import concourse.bass as bass
from concourse import mybir

ALU = mybir.AluOpType
ACT = mybir.ActivationFunctionType
AX_X = mybir.AxisListType.X
F32 = mybir.dt.float32
F32R = mybir.dt.float32r
I32 = mybir.dt.int32

P = 128
EPS = 1e-5


def audio_tower(nc, x, tok_w, tok_b, tok_gamma, tok_beta, w_ih, w_hh, b_ih, b_hh, w_out, b_out,
                gate_w, thr_w, fc1_w, lora_a, lora_b, fc2_w, out):
    B, T, D = x.shape
    FEAT, PATCH = tok_w.shape
    CONTEXT = PATCH // D
    HID = w_hh.shape[0]
    KH = HID // P
    E, R = lora_a.shape[0], lora_a.shape[2]
    L = T - CONTEXT + 1
    CHUNKS = P // B
    G = 4
    STEPS = -(-L // (CHUNKS * G)) * G
    GROUPS = STEPS // G
    WARM = 20
    LAST = L - (CHUNKS - 1) * STEPS
    W = G * P
    XW = (G + CONTEXT - 1) * D
    ER = 32
    FULL = LAST // G
    CUT = LAST % G
    FIRST = GROUPS - WARM // G
    TOL = 2.0 ** -20
    assert KH == 2 and FEAT == P and E * ER == P and GROUPS % 2 == 0 and WARM % G == 0
    assert FULL % 2 == 0 and 0 < CUT < G and 2 * (WARM // G + 1) == GROUPS >= 6
    COLS = (CHUNKS - 1) * B

    with ExitStack() as ctx:
        def sb(name, shape, dt=F32):
            return ctx.enter_context(nc.sbuf_tensor(name, shape, dt))

        def sem(name):
            return ctx.enter_context(nc.semaphore(name))

        ident = sb("ident", [P, P])
        lora_a_sb = sb("lora_a_sb", [P, E, ER])
        tokw_t = sb("tokw_t", [PATCH, P])
        tok_bias = sb("tok_bias", [P, 1])
        vecs = sb("vecs", [P, 8])
        bias_h = sb("bias_h", [P, KH])
        wih_t = sb("wih_t", [P, KH * P])
        wout_hi = sb("wout_hi", [P, KH * P], F32R)
        wout_lo = sb("wout_lo", [P, KH * P], F32R)
        wih_hi = sb("wih_hi", [P, KH * P], F32R)
        wih_lo = sb("wih_lo", [P, KH * P], F32R)
        whh_t = sb("whh_t", [P, KH * KH * P])
        wout_t = sb("wout_t", [P, KH * P])
        fc1_hi = sb("fc1_hi", [P, E * P], F32R)
        fc1_lo = sb("fc1_lo", [P, E * P], F32R)
        fc2_t = sb("fc2_t", [P, E * P])
        gate_t = sb("gate_t", [P, ER])
        lorab_t = sb("lorab_t", [P, E, ER])
        adapt = sb("adapt", [P, P])

        y_sb = sb("y_sb", [P, GROUPS * W])
        bn_st = sb("bn_st", [P, GROUPS + 1, 6])
        bn_mv = sb("bn_mv", [P, 2])
        bn_tmp = sb("bn_tmp", [P, 2])
        bn_ab = sb("bn_ab", [P, 3])
        half_neg = sb("half_neg", [P, G])
        hb = sb("hb", [P, 2, W])
        ln_st = sb("ln_st", [P, 2, G, 6])
        ln_mv = sb("ln_mv", [P, 2, G, 2])
        ln_ve = sb("ln_ve", [P, 2, G])
        ln_rs = sb("ln_rs", [P, 2, G])
        z_sb = sb("z_sb", [P, 2, W])
        h_tok = sb("h_tok", [P, GROUPS * W])
        a_in = sb("a_in", [P, GROUPS * W])
        state = sb("state", [P, KH, STEPS + 1, P])

        def h2_rows(g):
            return state[:, 0, bass.ds(G * g + 1, G), :]

        def z2_cols(g):
            return y_sb[:, bass.ds(g * W, W)]

        h_feat = sb("h_feat", [P, W])
        z_feat = sb("z_feat", [P, 2, W])
        part_hi = sb("part_hi", [P, 2, W], F32R)
        part_lo = sb("part_lo", [P, 2, W], F32R)
        logit_f = sb("logit_f", [P, P])
        g_in = sb("g_in", [P, G, E + 1])
        g_exp = sb("g_exp", [P, G, E + 1])
        g_max = sb("g_max", [P, G])
        g_den = sb("g_den", [P, 2, G])
        g_inv = sb("g_inv", [P, 2, G])
        g_p = sb("g_p", [P, G, E])
        g_w = sb("g_w", [P, G, E])
        g_wr = sb("g_wr", [P, G, E])
        g_sum = sb("g_sum", [P, G])
        g_sum1 = sb("g_sum1", [P, G])
        g_ws = sb("g_ws", [P, G])
        w_wide = sb("w_wide", [P, G, E, ER])
        hidden = sb("hidden", [P, 2, E, W])
        o_sb = sb("o_sb", [P, 2, W])

        diff = sb("diff", [P, KH, P])
        agree = sb("agree", [P, 1])
        cmp_col = sb("cmp_col", [P, 4])
        ok_f = sb("ok_f", [1, 1])
        ok_i = sb("ok_i", [1, 1], I32)

        with ExitStack() as early:
            def early_sb(name, shape):
                return early.enter_context(nc.sbuf_tensor(name, shape, F32))

            tokw_raw = early_sb("tokw_raw", [P, PATCH])
            vec_raw = early_sb("vec_raw", [8, P])
            tokb_raw = early_sb("tokb_raw", [1, P])
            wih_raw = early_sb("wih_raw", [P, KH, P])
            whh_raw = early_sb("whh_raw", [P, KH, HID])
            wout_raw = early_sb("wout_raw", [P, HID])
            fc1_raw = early_sb("fc1_raw", [P, E, P])
            fc2_raw = early_sb("fc2_raw", [P, E, P])
            gate_raw = early_sb("gate_raw", [ER, P])
            lorab_raw = early_sb("lorab_raw", [E * R, P])
            x_sb = early_sb("x_sb", [P, (STEPS + CONTEXT - 1) * D])
            x_piece = early_sb("x_piece", [P, 2, XW])
            patch_t = early_sb("patch_t", [PATCH, 2, W])
        state_hi = sb("state_hi", [P, KH, W], F32R)
        state_lo = sb("state_lo", [P, KH, W], F32R)
        w_feat = sb("w_feat", [P, W])
        low = sb("low", [P, W])

        bank = [ctx.enter_context(nc.psum_tensor(f"bank{i}", [P, W], F32)) for i in range(8)]

        names = """ident_zero ident_made x_landed x_landed2 tok_landed vec_landed rnn_landed fc1_landed ffn_landed
            zeroed x_zeroed vec_zeroed prep_done prep_copied adapt_done
            piece_ready patch_done patch_copied y_done y_ready bn_stats_done bn_step bn_pool
            head_step head_kept hb_ready h_done h_stats h_kept ln_mv_ready ln_step z_ready z_done a_ready
            state_hi_ready0 state_hi_ready1 state_lo_ready0 state_lo_ready1
            rnn_hi_ready rnn_split in_hi_ready in_lo_ready in_used pre0 pre1 state0 state1
            diff_done diff_turned cmp_step cmp_turned ok_ready redo_pre redo_state
            wout_done hf_ready h2_done h2_ready h2_stats mv2_ready ln2_step z2_ready z2_done zf_ready
            fc1_split zc_ready zhi_ready zlo_ready gate_done logit_ready logit_turned gate_step gate_sum exp_ready w_ready w_turned
            wf_ready fc1_done hidden_act hidden_dve low_done low_ready mix_done out_ready
            stored0 stored1 stored_cut
            first_low first_weighed first_mixed first_out first_stored"""
        S = {n: sem(n) for n in names.split()}

        def wait_past(eng, name, value):
            if not (isinstance(value, int) and value <= 0):
                eng.wait_ge(S[name], value)

        def wait_apart(eng, name, value):
            if not (isinstance(value, int) and value <= 0):
                eng.wait_ge(S[name], value)
                eng.nop(nofuse=True)

        def by_step(ap):
            return ap.rearrange("p (j c) -> p j c", j=G)

        def group_of(u):
            return (u + FIRST) % GROUPS

        def one(j):
            return slice(j * P, (j + 1) * P)

        rb = [[bank[0], bank[1]], [bank[2], bank[3]]]
        h_bank, z_bank = bank[4:6], bank[6:8]
        wo_bank, h2_bank, z2_bank = bank[4], bank[5], bank[6]
        fc_bank, low_bank, w_bank, mix_bank, gate_bank = bank[0:2], bank[2], bank[3], bank[4], bank[7]
        cmp_bank = bank[5]

        prep = [
            (0, [(tokw_raw[:, :], P, PATCH), (tokb_raw[:, :], 1, P)], [("tok_landed", 2)]),
            (0, [(wih_raw[:, m, :], P, P) for m in range(KH)] + [(vec_raw[:, :], 8, P)],
             [("rnn_landed", 2), ("vec_landed", 5)]),
            (3, [(fc1_raw[:, e, :], P, P) for e in range(E)], [("fc1_landed", 1)]),
            (1, [(whh_raw[:, m, k * P:(k + 1) * P], P, P) for m in range(KH) for k in range(KH)], []),
            (2, [(wout_raw[:, k * P:(k + 1) * P], P, P) for k in range(KH)]
             + [(gate_raw[:, :], ER, P), (lorab_raw[:, :], E * R, P)], [("ffn_landed", 6)]),
            (6, [(fc2_raw[:, e, :], P, P) for e in range(E)], []),
        ]
        PREP_TOK, PREP_IH, PREP_FC1, PREP_HH, PREP_OUT, PREP_FC2 = range(1, len(prep) + 1)

        HEAD_HB, HEAD_TURNED, HEAD_STATS, HEAD_MOMENTS, HEAD_VAR, HEAD_RS, HEAD_Z, HEAD_BACK, HEAD_A = range(1, 10)
        head_bank = bank[7]

        WHOLE = 3
        WARMUPS = WARM // G
        SPLITS = WARMUPS - WHOLE + GROUPS

        HEAD_PARITY = (WARMUPS + 1) % 2

        def split_of(g):
            return g + WARMUPS - WHOLE

        H = W // 2
        tail = [(slice(0, H), bank[2], bank[4]), (slice(H, W), bank[7], bank[5])]

        block = ctx.enter_context(nc.Block())

        @block.sync
        def _(sp):
            rows = STEPS + CONTEXT - 1
            early = (2 * G + CONTEXT - 1) * D

            def x_rows(a, b):
                sp.dma_start(x_sb[0:COLS, a:b], bass.AP(tensor=x.tensor, offset=a,
                             ap=[[STEPS * D, CHUNKS - 1], [T * D, B], [1, b - a]]))\
                    .then_inc(S["x_landed" if a == 0 else "x_landed2"], 16)

            x_rows(0, early)
            sp.dma_start(tokw_raw[:, :], tok_w).then_inc(S["tok_landed"], 16)
            sp.wait_ge(S["x_zeroed"], 1)
            sp.dma_start(x_sb[COLS:P, 0:(LAST + CONTEXT - 1) * D],
                         bass.AP(tensor=x.tensor, offset=(CHUNKS - 1) * STEPS * D,
                                 ap=[[T * D, B], [1, (LAST + CONTEXT - 1) * D]])).then_inc(S["x_landed"], 16)
            x_rows(early, rows * D)
            sp.dma_start(wih_raw[:, :, :], w_ih.rearrange("(m h) i -> h m i", m=KH)).then_inc(S["rnn_landed"], 16)
            sp.dma_start(whh_raw[:, :, :], w_hh.rearrange("(m h) i -> h m i", m=KH)).then_inc(S["rnn_landed"], 16)
            sp.wait_ge(S["vec_zeroed"], 1)
            for r, v in ((4, b_ih), (6, b_hh)):
                sp.dma_start(vec_raw[r:r + 2, :], v.rearrange("(m h) -> m h", m=KH))\
                    .then_inc(S["vec_landed"], 16)
            for r, v in ((0, tok_gamma), (1, tok_beta), (2, b_out)):
                sp.dma_start(vec_raw[r:r + 1, :], v.rearrange("(a d) -> a d", a=1)).then_inc(S["vec_landed"], 16)
            sp.dma_start(fc1_raw[:, :, :], fc1_w.rearrange("e h i -> h e i")).then_inc(S["fc1_landed"], 16)
            sp.dma_start(fc2_raw[:, :, :], fc2_w.rearrange("e d o -> d e o")).then_inc(S["ffn_landed"], 16)
            sp.dma_start(wout_raw[:, :], w_out).then_inc(S["ffn_landed"], 16)
            sp.wait_ge(S["zeroed"], 1)
            sp.dma_start(gate_raw[0:E, :], gate_w).then_inc(S["ffn_landed"], 16)
            sp.dma_start(gate_raw[E:E + 1, :], thr_w).then_inc(S["ffn_landed"], 16)
            sp.dma_start(lora_a_sb[:, :, 0:R], lora_a.rearrange("e h r -> h e r")).then_inc(S["ffn_landed"], 16)
            sp.dma_start(lorab_raw[:, :], lora_b.rearrange("e r o -> (e r) o")).then_inc(S["ffn_landed"], 16)

            def store(c0, n_chunks, g, half, steps, name, j0=0):
                sp.dma_start(
                    bass.AP(tensor=out.tensor, offset=(c0 * STEPS + G * g + j0) * P,
                            ap=[[STEPS * P, n_chunks], [L * P, B], [1, steps * P]]),
                    o_sb[c0 * B:(c0 + n_chunks) * B, half, j0 * P:(j0 + steps) * P]).then_inc(S[name], 16)

            def store_all(n0):
                with sp.Fori(0, FULL // 2) as p:
                    for half in range(2):
                        sp.wait_ge(S["out_ready"], n0 + 2 * p + half + 1)
                        store(0, CHUNKS, 2 * p + half, half, G, f"stored{half}")
                sp.wait_ge(S["out_ready"], n0 + FULL + 1)
                store(CHUNKS - 1, 1, FULL, 0, CUT, "stored_cut")
                sp.wait_ge(S["stored_cut"], 16 * (n0 // GROUPS + 1))
                store(0, CHUNKS - 1, FULL, 0, G, "stored0")
                sp.wait_ge(S["out_ready"], n0 + FULL + 2)
                store(0, CHUNKS - 1, FULL + 1, 1, G, "stored1")
                for g in range(FULL + 2, GROUPS - 1):
                    sp.wait_ge(S["out_ready"], n0 + g + 1)
                    store(0, CHUNKS - 1, g, g % 2, G, f"stored{g % 2}")
                sp.wait_ge(S["first_out"], n0 // GROUPS + 1)
                store(0, CHUNKS - 1, GROUPS - 1, 1, G // 2, "first_stored")
                sp.wait_ge(S["out_ready"], n0 + GROUPS)
                store(0, CHUNKS - 1, GROUPS - 1, 1, G // 2, "stored1", j0=G // 2)
                sp.wait_ge(S["first_stored"], 16 * (n0 // GROUPS + 1))
                for half in range(2):
                    sp.wait_ge(S[f"stored{half}"], 16 * (n0 + GROUPS) // 2)

            store_all(0)
            sp.wait_ge(S["ok_ready"], 1)
            ok = sp.value_load(ok_i[0:1, 0:1], min_val=0, max_val=1)
            with sp.If(ok == 0):
                store_all(GROUPS)
            sp.end_ifs()

        @block.gpsimd
        def _(pool):
            nc.gpsimd.memset(ident[:, :], 0.0).then_inc(S["ident_zero"], 1)
            pool.wait_ge(S["ident_zero"], 1)
            nc.gpsimd.affine_select(out=ident[:, :], in_=ident[:, :], compare_op=ALU.not_equal, fill=1.0,
                                    base=0, pattern=[[-1, P]], channel_multiplier=1).then_inc(S["ident_made"], 1)
            nc.gpsimd.memset(half_neg[:, :], -0.5)

            def piece(g, half):
                nc.gpsimd.tensor_copy(x_piece[:, half, :], x_sb[:, bass.ds(g * (G * D), XW)])\
                    .then_inc(S["piece_ready"], 1)

            pool.wait_ge(S["x_landed"], 32)
            pool.wait_ge(S["x_landed2"], 16)
            piece(2, 0)
            piece(3, 1)
            with pool.Fori(2, GROUPS // 2) as p:
                for half in range(2):
                    pool.wait_ge(S["patch_done"], 2 * p + (half - 1))
                    piece(2 * p + half, half)

            pool.wait_ge(S["bn_step"], 1)
            nc.gpsimd.tensor_scalar(bn_tmp[:, 0:1], bn_mv[:, 1:2], EPS, None, ALU.add).then_inc(S["bn_pool"], 1)
            pool.wait_ge(S["bn_pool"], 1)
            nc.gpsimd.tensor_tensor(bn_tmp[:, 1:2], bn_tmp[:, 0:1], half_neg[:, 0:1], ALU.pow)\
                .then_inc(S["bn_pool"], 1)

            def inverse_std(half, ready, n, step, j0=0):
                wait_apart(pool, ready, n + 1)
                nc.gpsimd.tensor_scalar(ln_ve[:, half, j0:], ln_mv[:, half, j0:, 1], EPS, None, ALU.add)\
                    .then_inc(S[step], 1)
                pool.wait_ge(S[step], 2 * n + 1)
                nc.gpsimd.tensor_tensor(ln_rs[:, half, j0:], ln_ve[:, half, j0:], half_neg[:, j0:], ALU.pow)\
                    .then_inc(S[step], 1)

            pool.wait_ge(S["head_step"], HEAD_MOMENTS)
            nc.gpsimd.tensor_scalar(ln_ve[:, 0, 0:1], ln_mv[:, 0, 0:1, 1], EPS, None, ALU.add)\
                .then_inc(S["head_step"], 1)
            pool.wait_ge(S["head_step"], HEAD_VAR)
            nc.gpsimd.tensor_tensor(ln_rs[:, 0, 0:1], ln_ve[:, 0, 0:1], half_neg[:, 0:1], ALU.pow)\
                .then_inc(S["head_step"], 1)
            inverse_std(0, "ln_mv_ready", 0, "ln_step", j0=1)
            inverse_std(1, "ln_mv_ready", 1, "ln_step")

            def split_in(g, at, half):
                n = split_of(g)
                pool.wait_ge(S["in_hi_ready"], n + 1)
                wait_past(pool, "in_used", n - 1)
                nc.gpsimd.tensor_tensor(part_lo[:, half, :], a_in[:, bass.ds(at * W, W)],
                                        part_hi[:, half, :].bitcast(F32), ALU.subtract)\
                    .then_inc(S["in_lo_ready"], 1)

            for i in range(WARMUPS):
                for half in range(2):
                    inverse_std(half, "ln_mv_ready", 2 * i + 2 + half, "ln_step")
                if i == 0:
                    for n, (lo, full, hi) in enumerate(((wih_lo, wih_t, wih_hi), (wout_lo, wout_t, wout_hi))):
                        pool.wait_ge(S["rnn_hi_ready"], n + 1)
                        nc.gpsimd.tensor_tensor(lo[:, :], full[:, :], hi[:, :].bitcast(F32), ALU.subtract)\
                            .then_inc(S["rnn_split"], 1)
                else:
                    g = i + 2 - WARMUPS
                    split_in(g, g % GROUPS, g % 2)

            def z_copy(g, half, n):
                pool.wait_ge(S["zf_ready"], n + 1)
                wait_apart(pool, "gate_done", n - 1)
                nc.gpsimd.tensor_copy(z_feat[:, half, :], z2_cols(g)).then_inc(S["zc_ready"], 1)

            def split_state(q):
                for k in range(KH):
                    pool.wait_ge(S[f"state_hi_ready{k}"], q + 1)
                    wait_past(pool, "wout_done", q)
                    nc.gpsimd.tensor_tensor(by_step(state_lo[:, k, :]), state[:, k, bass.ds(G * q + 1, G), :],
                                            by_step(state_hi[:, k, :]).bitcast(F32), ALU.subtract)\
                        .then_inc(S[f"state_lo_ready{k}"], 1)

            split_in(2, 2, 0)
            split_state(0)
            split_in(3, 3, 1)
            with pool.Fori(1, GROUPS // 2 - 1) as p:
                for half in range(2):
                    split_state(2 * p + half - 1)
                    inverse_std(0, "mv2_ready", 2 * p + half - 2, "ln2_step")
                    split_in(2 * p + half + 2, 2 * p + half + 2, half)
            split_state(GROUPS - 3)
            inverse_std(0, "mv2_ready", GROUPS - 4, "ln2_step")
            split_state(GROUPS - 2)
            inverse_std(0, "mv2_ready", GROUPS - 3, "ln2_step")
            split_state(GROUPS - 1)
            for g in range(2, 5):
                z_copy(g, g % 2, g)
            inverse_std(0, "mv2_ready", GROUPS - 2, "ln2_step")
            z_copy(5, 1, 5)
            inverse_std(0, "mv2_ready", GROUPS - 1, "ln2_step")
            with pool.Fori(3, GROUPS // 2) as p:
                for half in range(2):
                    z_copy(2 * p + half, half, 2 * p + half)
            pool.wait_ge(S["ok_ready"], 1)
            ok = pool.value_load(ok_i[0:1, 0:1], min_val=0, max_val=1)
            with pool.If(ok == 0):
                with pool.Fori(0, GROUPS) as q:
                    inverse_std(0, "mv2_ready", GROUPS + q, "ln2_step")
                with pool.Fori(0, GROUPS // 2) as p:
                    for half in range(2):
                        z_copy(2 * p + half, half, GROUPS + 2 * p + half)
            pool.end_ifs()

        @block.scalar
        def _(act):
            act.dma_start(tokb_raw[:, :], tok_b.rearrange("(a d) -> a d", a=1)).then_inc(S["tok_landed"], 16)

            def copied(dst, src):
                return nc.scalar.activation(dst, src, ACT.Copy)

            act.wait_ge(S["vec_zeroed"], 1)
            nc.scalar.activation(g_max[:, 0:1], bn_tmp[:, 0:1], ACT.Exp)

            act.wait_ge(S["prep_copied"], PREP_TOK)
            with act.Fori(0, GROUPS // 2) as p:
                for half in range(2):
                    act.wait_ge(S["y_done"], 2 * p + half + 1)
                    nc.scalar.activation(y_sb[:, bass.ds((2 * p + half) * W, W)], bank[6 + half][:, :],
                                         ACT.Relu, bias=tok_bias[:, 0:1]).then_inc(S["y_ready"], 1)

            act.wait_ge(S["prep_done"], PREP_IH)
            copied(vecs[:, :], bank[0][:, KH * P:KH * P + 8])
            copied(wih_t[:, :], bank[0][:, 0:KH * P]).then_inc(S["prep_copied"], 1)
            act.wait_ge(S["prep_done"], PREP_FC1)
            copied(fc1_hi[:, :], bank[3][:, :]).then_inc(S["prep_copied"], 1)
            act.wait_ge(S["prep_done"], PREP_HH)
            copied(whh_t[:, :], bank[1][:, :]).then_inc(S["prep_copied"], 1)

            def bn_apply(u, half, j0=0, signal="hb_ready", j1=G):
                if not (isinstance(u, int) and u < 2):
                    act.wait_ge(S["h_done"], u - 1)
                nc.scalar.activation(hb[:, half, j0 * P:j1 * P],
                                     y_sb[:, bass.ds(group_of(u) * W + j0 * P, (j1 - j0) * P)], ACT.Identity,
                                     bias=bn_ab[:, 2:3], scale=bn_ab[:, 0:1]).then_inc(S[signal], 1)

            def keep_rows(u, half, j0=0):
                act.wait_ge(S["h_stats"], u + 1)
                copied(h_tok[:, bass.ds(group_of(u) * W + j0 * P, W - j0 * P)], h_bank[half][:, j0 * P:])\
                    .then_inc(S["h_kept"], 1)

            def keep_normed(u, half, j0=0):
                act.wait_ge(S["z_done"], u + 1)
                copied(a_in[:, bass.ds(group_of(u) * W + j0 * P, W - j0 * P)], z_bank[half][:, j0 * P:])\
                    .then_inc(S["a_ready"], 1)

            act.wait_ge(S["prep_done"], PREP_OUT)
            copied(wout_t[:, :], bank[2][:, 0:KH * P])
            copied(gate_t[:, :], bank[2][:, 2 * P:2 * P + ER])
            copied(lorab_t[:, :, 0:R], bank[2][:, 3 * P:3 * P + E * R].rearrange("p (e r) -> p e r", e=E))\
                .then_inc(S["prep_copied"], 1)
            act.wait_ge(S["prep_done"], PREP_FC2)
            copied(fc2_t[:, :], bank[6][:, :]).then_inc(S["prep_copied"], 1)
            act.wait_ge(S["bn_step"], 4)
            bn_apply(0, 0, signal="head_step", j1=1)
            bn_apply(0, 0, j0=1)
            act.wait_ge(S["prep_done"], len(prep) + 1)
            copied(adapt[:, :], h_bank[1][:, 0:P]).then_inc(S["adapt_done"], 1)
            bn_apply(1, 1)
            act.wait_ge(S["head_step"], HEAD_Z)
            head_cols = slice(FIRST * W, FIRST * W + P)
            copied(h_tok[:, head_cols], head_bank[:, 0:P]).then_inc(S["head_kept"], 1)
            keep_rows(0, 0, j0=1)
            act.wait_ge(S["head_step"], HEAD_BACK)
            copied(a_in[:, head_cols], z_bank[0][:, 0:P]).then_inc(S["head_step"], 1)
            keep_rows(1, 1)
            bn_apply(2, 0)

            def relu1(n, slot, a, parity, j, cols):
                act.wait_ge(S["pre1"], n + 1)
                nc.scalar.activation(state[:, 1, slot, a:a + cols], rb[1][parity][:, j * P:j * P + cols],
                                     ACT.Relu, bias=bias_h[:, 1:2]).then_inc(S["state1"], 1)

            def split_in(g, at, half):
                if isinstance(g, int):
                    act.wait_ge(S["a_ready"], min(g + WARMUPS + 1, GROUPS))
                wait_past(act, "in_used", split_of(g) - 1)
                copied(part_hi[:, half, :], a_in[:, bass.ds(at * W, W)]).then_inc(S["in_hi_ready"], 1)


            for i in range(WARMUPS):
                a, b = 2 * i + 2, 2 * i + 3
                parity = (i - WARMUPS) % 2
                if i == 0:
                    relu1(0, 1, B, HEAD_PARITY, 0, COLS)
                    keep_normed(0, 0, j0=1)
                    copied(wih_hi[:, :], wih_t[:, :]).then_inc(S["rnn_hi_ready"], 1)
                    copied(wout_hi[:, :], wout_t[:, :]).then_inc(S["rnn_hi_ready"], 1)
                else:
                    keep_normed(a - 2, 0)
                    relu1(G * i, 1, B, parity, 0, COLS)
                bn_apply(b, 1)
                relu1(G * i + 1, 0, B, parity, 1, COLS)
                keep_rows(a, 0)
                if i < WARMUPS - 1:
                    bn_apply(a + 2, 0)
                relu1(G * i + 2, 1, B, parity, 2, COLS)
                keep_normed(b - 2, 1)
                keep_rows(b, 1)
                relu1(G * i + 3, 0, B, parity, 3, COLS)
                if i >= 1:
                    g = i + 2 - WARMUPS
                    split_in(g, g % GROUPS, g % 2)

            def attn_out(n):
                act.wait_ge(S["wout_done"], n + 1)
                wait_past(act, "h2_done", n)
                nc.scalar.activation(h_feat[:, :], wo_bank[:, :], ACT.Identity, bias=vecs[:, 2:3])\
                    .then_inc(S["hf_ready"], 1)

            def keep_z2(q, n):
                act.wait_ge(S["z2_done"], n + 1)
                copied(z2_cols(q), z2_bank[:, :]).then_inc(S["zf_ready"], 1)

            def split_state(q):
                wait_past(act, "wout_done", q)
                for k in range(KH):
                    wait_apart(act, f"state{k}", WARM + G * (q + 1) + 1)
                    nc.scalar.activation(by_step(state_hi[:, k, :]), state[:, k, bass.ds(G * q + 1, G), :],
                                         ACT.Copy).then_inc(S[f"state_hi_ready{k}"], 1)

            def main(g, parity):
                first = isinstance(g, int)
                for j in range(G):
                    if j == 2 and (not first or g + 2 < GROUPS):
                        split_in(g + 2, g + 2, parity)
                    if first and g == 0:
                        if j == 1:
                            keep_normed(GROUPS - 2, 0)
                        elif j == 3:
                            keep_normed(GROUPS - 1, 1)
                    elif j == 0:
                        split_state(g - 1)
                    if j == 1 and (not first or g >= 3):
                        keep_z2(g - 3, g - 3)
                    if j == 3 and (not first or g >= 1):
                        attn_out(g - 1)
                    if first and g == GROUPS - 1:
                        if j == 1:
                            act.wait_ge(S["in_used"], SPLITS)
                            split_z(0, 0, 0)
                            logits(0)
                        elif j == 3:
                            exponentials(0)
                    relu1(WARM + G * g + j, bass.ds(G * g + j + 1, 1), 0, parity, j, P)

            def logits(n):
                act.wait_ge(S["gate_done"], n + 1)
                wait_past(act, "logit_turned", n)
                copied(logit_f[:, :], gate_bank[:, 0:P]).then_inc(S["logit_ready"], 1)

            def unit(n, e, half):
                act.wait_ge(S["fc1_done"], E * n + e + 1)
                wait_past(act, "low_done", n - 1)
                nc.scalar.activation(hidden[:, half, e, :], fc_bank[e % 2][:, :], ACT.Relu)\
                    .then_inc(S["hidden_act"], 1)

            def spread_w(n):
                act.wait_ge(S["w_turned"], n + 1)
                wait_past(act, "low_ready", n)
                copied(w_feat[:, :], w_bank[:, :]).then_inc(S["wf_ready"], 1)

            def split_z(g, n, half):
                act.wait_ge(S["zf_ready"], n + 1)
                wait_past(act, "fc1_done", E * (n - 1))
                copied(part_hi[:, half, :], z2_cols(g)).then_inc(S["zhi_ready"], 1)

            def exponentials(n):
                act.wait_ge(S["gate_step"], 10 * n + 3)
                nc.scalar.activation(g_exp[:, :, :], g_in[:, :, :], ACT.Exp).then_inc(S["exp_ready"], 1)

            def widen_w(n):
                act.wait_ge(S["gate_step"], 10 * n + 10)
                wait_past(act, "w_turned", n)
                for j in range(G):
                    last = nc.scalar.activation(
                        w_wide[:, j, :, :], g_wr[:, j, :].unsqueeze(2).to_broadcast([P, E, ER]),
                        ACT.Copy, scale=g_ws[:, j:j + 1])
                last.then_inc(S["w_ready"], 1)

            def group(g, n, half, left=2, hook=None, end=None):
                unit(n, 0, half)
                widen_w(n)
                if left >= 1:
                    exponentials(n + 1)
                    split_z(g + 1, n + 1, 1 - half)
                unit(n, 2, half)
                spread_w(n)
                if hook:
                    hook()
                unit(n, 3, half)
                if left >= 2:
                    logits(n + 2)
                if end:
                    end()

            def experts(n0, hooks):
                logits(n0 + 1)
                for g in range(4):
                    group(g, n0 + g, g % 2, **hooks.get(g, {}))
                with act.Fori(2, GROUPS // 2 - 1) as p:
                    for half in range(2):
                        group(2 * p + half, n0 + 2 * p + half, half)
                group(GROUPS - 2, n0 + GROUPS - 2, 0, left=1)
                group(GROUPS - 1, n0 + GROUPS - 1, 1, left=0)

            for g in range(4):
                main(g, g % 2)
            with act.Fori(2, GROUPS // 2 - 1) as p:
                for parity in range(2):
                    main(2 * p + parity, parity)
            for g in (GROUPS - 2, GROUPS - 1):
                main(g, g % 2)
            split_state(GROUPS - 1)
            keep_z2(GROUPS - 3, GROUPS - 3)
            experts(0, {0: {"hook": lambda: attn_out(GROUPS - 1)},
                        2: {"end": lambda: keep_z2(GROUPS - 2, GROUPS - 2)},
                        3: {"end": lambda: keep_z2(GROUPS - 1, GROUPS - 1)}})
            act.wait_ge(S["ok_ready"], 1)
            ok = act.value_load(ok_i[0:1, 0:1], min_val=0, max_val=1)
            with act.If(ok == 0):
                with act.Fori(0, GROUPS) as q:
                    attn_out(GROUPS + q)
                    keep_z2(q, GROUPS + q)
                split_z(0, GROUPS, 0)
                logits(GROUPS)
                exponentials(GROUPS)
                experts(GROUPS, {})
            act.end_ifs()

        @block.vector
        def _(dve):
            nc.vector.memset(bn_tmp[:, :], 0.0)
            nc.vector.memset(x_sb[96:P, (LAST + CONTEXT - 1) * D:], 0.0).then_inc(S["x_zeroed"], 1)
            nc.vector.memset(vec_raw[:, :], 0.0).then_inc(S["vec_zeroed"], 1)
            nc.vector.memset(gate_raw[:, :], 0.0)
            nc.vector.memset(lora_a_sb[:, :, :], 0.0)
            nc.vector.memset(lorab_t[:, :, :], 0.0).then_inc(S["zeroed"], 1)
            for k in range(KH):
                nc.vector.memset(state[:, k, 0:2, :], 0.0).then_inc(S[f"state{k}"], 1)

            def patch_copy(g, half):
                dve.wait_ge(S["patch_done"], g + 1)
                wait_past(dve, "y_done", g - 1)
                nc.vector.tensor_copy(patch_t[:, half, :], bank[4 + half][0:PATCH, :])\
                    .then_inc(S["patch_copied"], 1)

            def stats(g):
                wait_apart(dve, "y_ready", g + 1)
                nc.vector.bn_stats(bn_st[:, bass.ds(g, 1), :], y_sb[:, bass.ds(g * W, W)])\
                    .then_inc(S["bn_stats_done"], 1)

            def stats_short(g):
                wait_apart(dve, "y_ready", g + 1)
                nc.vector.bn_stats(bn_st[:, g, :], by_step(y_sb[:, g * W:(g + 1) * W])[:, :, 0:COLS])\
                    .then_inc(S["bn_stats_done"], 1)

            def stats_cut(g):
                dve.wait_ge(S["y_ready"], g + 1)
                nc.vector.bn_stats(bn_st[:, g, :], y_sb[:, g * W:g * W + CUT * P])
                nc.vector.bn_stats(bn_st[:, GROUPS, :], by_step(y_sb[:, g * W:(g + 1) * W])[:, CUT:G, 0:COLS])\
                    .then_inc(S["bn_stats_done"], 1)

            dve.wait_ge(S["prep_done"], PREP_TOK)
            nc.vector.tensor_copy(tokw_t[:, :], bank[0][0:PATCH, 0:P])
            nc.vector.tensor_copy(tok_bias[:, :], bank[0][:, P:P + 1]).then_inc(S["prep_copied"], 1)
            patch_copy(0, 0)
            patch_copy(1, 1)
            with dve.Fori(1, FULL // 2 + 1) as p:
                for half in range(2):
                    patch_copy(2 * p + half, half)
                    stats(2 * p + half - 2)
            for g in range(FULL + 2, GROUPS + 2):
                if g < GROUPS:
                    patch_copy(g, g % 2)
                (stats_cut if g - 2 == FULL else stats_short)(g - 2)

            dve.wait_ge(S["bn_stats_done"], GROUPS)
            nc.vector.bn_aggr(bn_mv[:, :], bn_st[:, :, :]).then_inc(S["bn_step"], 1)
            dve.wait_ge(S["prep_copied"], PREP_IH)
            nc.vector.tensor_tensor(bias_h[:, :], vecs[:, 4:6], vecs[:, 6:8], ALU.add)
            dve.wait_ge(S["prep_copied"], PREP_FC1)
            nc.vector.tensor_tensor(fc1_lo[:, :], bank[3][:, :], fc1_hi[:, :].bitcast(F32), ALU.subtract)\
                .then_inc(S["fc1_split"], 1)
            dve.wait_ge(S["bn_pool"], 2)
            nc.vector.tensor_tensor(bn_ab[:, 0:1], vecs[:, 0:1], bn_tmp[:, 1:2], ALU.mult).then_inc(S["bn_step"], 1)
            dve.wait_ge(S["bn_step"], 2)
            nc.vector.tensor_tensor(bn_ab[:, 1:2], bn_mv[:, 0:1], bn_ab[:, 0:1], ALU.mult).then_inc(S["bn_step"], 1)
            dve.wait_ge(S["bn_step"], 3)
            nc.vector.tensor_tensor(bn_ab[:, 2:3], vecs[:, 1:2], bn_ab[:, 1:2], ALU.subtract)\
                .then_inc(S["bn_step"], 1)

            def ln1_stats(u, half, j0=0):
                wait_apart(dve, "h_done", u + 1)
                for j in range(j0, G):
                    last = nc.vector.bn_stats(ln_st[:, half, j, :], h_bank[half][:, one(j)])
                last.then_inc(S["h_stats"], 1)

            def ln1_moments(u, half, j0=0):
                wait_apart(dve, "h_stats", u + 1)
                for j in range(j0, G):
                    last = nc.vector.bn_aggr(ln_mv[:, half, j, :], ln_st[:, half, j, :])
                last.then_inc(S["ln_mv_ready"], 1)

            def ln1_norm(u, half, j0=0):
                dve.wait_ge(S["ln_step"], 2 * u + 2)
                dve.wait_ge(S["h_kept"], u + 1)
                wait_past(dve, "z_done", u - 1)
                for j in range(j0, G):
                    last = nc.vector.tensor_scalar(
                        z_sb[:, half, one(j)], h_tok[:, bass.ds(group_of(u) * W + j * P, P)],
                        ln_mv[:, half, j, 0:1], ln_rs[:, half, j:j + 1], ALU.subtract, ALU.mult)
                last.then_inc(S["z_ready"], 1)

            def relu0(n, slot, a, parity, j, cols):
                dve.wait_ge(S["pre0"], n + 1)
                nc.vector.tensor_scalar(state[:, 0, slot, a:a + cols], rb[0][parity][:, j * P:j * P + cols],
                                        bias_h[:, 0:1], 0.0, ALU.add, ALU.max).then_inc(S["state0"], 1)

            dve.wait_ge(S["head_step"], HEAD_TURNED)
            nc.vector.bn_stats(ln_st[:, 0, 0, :], head_bank[:, 0:P]).then_inc(S["head_step"], 1)
            dve.wait_ge(S["head_step"], HEAD_STATS)
            nc.vector.bn_aggr(ln_mv[:, 0, 0, :], ln_st[:, 0, 0, :]).then_inc(S["head_step"], 1)
            ln1_stats(0, 0, j0=1)
            ln1_moments(0, 0, j0=1)
            dve.wait_ge(S["head_step"], HEAD_RS)
            nc.vector.tensor_scalar(z_sb[:, 0, 0:P], head_bank[:, 0:P], ln_mv[:, 0, 0, 0:1], ln_rs[:, 0, 0:1],
                                    ALU.subtract, ALU.mult).then_inc(S["head_step"], 1)
            ln1_stats(1, 1)
            ln1_norm(0, 0, j0=1)
            ln1_moments(1, 1)

            for i in range(WARMUPS):
                a, b = 2 * i + 2, 2 * i + 3
                parity = (i - WARMUPS) % 2
                relu0(G * i, 1, B, HEAD_PARITY if i == 0 else parity, 0, COLS)
                if i == 0:
                    ln1_norm(1, 1)
                ln1_stats(a, 0)
                relu0(G * i + 1, 0, B, parity, 1, COLS)
                ln1_moments(a, 0)
                ln1_stats(b, 1)
                relu0(G * i + 2, 1, B, parity, 2, COLS)
                ln1_moments(b, 1)
                ln1_norm(a, 0)
                relu0(G * i + 3, 0, B, parity, 3, COLS)
                ln1_norm(b, 1)

            def h2(q, n):
                dve.wait_ge(S["h2_done"], n + 1)
                nc.vector.tensor_tensor(h2_rows(q), by_step(h2_bank[:, :]), by_step(h_tok[:, bass.ds(q * W, W)]),
                                        ALU.add).then_inc(S["h2_ready"], 1)

            def h2_stats(q, n):
                wait_apart(dve, "h2_ready", n + 1)
                for j in range(G):
                    last = nc.vector.bn_stats(ln_st[:, 0, j, :], state[:, 0, bass.ds(G * q + j + 1, 1), :])
                last.then_inc(S["h2_stats"], 1)

            def h2_moments(n):
                wait_apart(dve, "h2_stats", n + 1)
                for j in range(G):
                    last = nc.vector.bn_aggr(ln_mv[:, 0, j, :], ln_st[:, 0, j, :])
                last.then_inc(S["mv2_ready"], 1)

            def h2_norm(q, n):
                dve.wait_ge(S["ln2_step"], 2 * n + 2)
                wait_past(dve, "z2_done", n)
                for j in range(G):
                    last = nc.vector.tensor_scalar(
                        z_sb[:, 0, one(j)], state[:, 0, bass.ds(G * q + j + 1, 1), :],
                        ln_mv[:, 0, j, 0:1], ln_rs[:, 0, j:j + 1], ALU.subtract, ALU.mult)
                last.then_inc(S["z2_ready"], 1)

            def main(g, parity):
                first = isinstance(g, int)
                for j in range(G):
                    relu0(WARM + G * g + j, bass.ds(G * g + j + 1, 1), 0, parity, j, P)
                    if first and g == GROUPS - 2 and j % 2 == 1:
                        dve.wait_ge(S["zf_ready"], j // 2 + 1)
                        nc.vector.tensor_copy(z_feat[:, j // 2, :], z2_cols(j // 2)).then_inc(S["zc_ready"], 1)
                    if j == 3 and (not first or g >= 1):
                        h2(g - 1, g - 1)
                    if not first or g >= 2:
                        if j == 0:
                            h2_stats(g - 2, g - 2)
                        if j == 1:
                            h2_moments(g - 2)
                        if j == 2:
                            h2_norm(g - 2, g - 2)
                    if first and g == GROUPS - 1:
                        if j == 1:
                            split_z(0, 0, 0)
                        elif j == 2:
                            gates_a(0)

            def over_experts(v, n):
                return v.unsqueeze(2).to_broadcast([P, G, n])

            def gates_a(n):
                dve.wait_ge(S["logit_turned"], n + 1)
                lg = gate_bank[:, P:2 * P].rearrange("p (j c) -> p j c", j=G)
                nc.vector.tensor_reduce(g_max[:, :], lg[:, :, 0:E], AX_X, ALU.max).then_inc(S["gate_step"], 1)
                nc.vector.tensor_scalar(g_in[:, :, E], lg[:, :, E], -1.0, None, ALU.mult).then_inc(S["gate_step"], 1)
                dve.wait_ge(S["gate_step"], 10 * n + 1)
                nc.vector.tensor_tensor(g_in[:, :, 0:E], lg[:, :, 0:E], over_experts(g_max[:, :], E),
                                        ALU.subtract).then_inc(S["gate_step"], 1)

            def gates_b(n):
                def step(k, instr):
                    instr.then_inc(S["gate_step"], 1)
                    dve.wait_ge(S["gate_step"], 10 * n + k)

                dve.wait_ge(S["exp_ready"], n + 1)
                nc.vector.tensor_reduce(g_den[:, 0, :], g_exp[:, :, 0:E], AX_X, ALU.add)
                step(4, nc.vector.tensor_scalar(g_den[:, 1, :], g_exp[:, :, E], float(E), float(E),
                                                ALU.mult, ALU.add))
                step(5, nc.vector.reciprocal(g_inv[:, :, :], g_den[:, :, :]))
                step(6, nc.vector.tensor_tensor(g_p[:, :, :], g_exp[:, :, 0:E],
                                                over_experts(g_inv[:, 0, :], E), ALU.mult))
                step(7, nc.vector.tensor_tensor(g_w[:, :, :], g_p[:, :, :],
                                                over_experts(g_inv[:, 1, :], E), ALU.subtract))
                wait_past(dve, "w_ready", n)
                step(8, nc.vector.tensor_scalar(g_wr[:, :, :], g_w[:, :, :], 0.0, None, ALU.max))
                step(9, nc.vector.tensor_reduce(g_sum[:, :], g_wr[:, :, :], AX_X, ALU.add))
                nc.vector.scalar_tensor_tensor(g_sum1[:, :], g_sum[:, :], 0.0, g_sum[:, :],
                                               ALU.is_equal, ALU.add).then_inc(S["gate_sum"], 1)
                dve.wait_ge(S["gate_sum"], n + 1)
                nc.vector.reciprocal(g_ws[:, :], g_sum1[:, :]).then_inc(S["gate_step"], 1)

            def unit(n, e, half):
                dve.wait_ge(S["fc1_done"], E * n + e + 1)
                wait_past(dve, "low_done", n - 1)
                nc.vector.tensor_scalar(hidden[:, half, e, :], fc_bank[e % 2][:, :], 0.0, None, ALU.max)\
                    .then_inc(S["hidden_dve"], 1)

            def weigh(n):
                dve.wait_ge(S["wf_ready"], n + 1)
                dve.wait_ge(S["low_done"], n + 1)
                wait_past(dve, "mix_done", n)
                nc.vector.tensor_tensor(low[:, :], low_bank[:, :], w_feat[:, :], ALU.mult).then_inc(S["low_ready"], 1)

            def add_up(g, n, half, earlier):
                dve.wait_ge(S["mix_done"], n + 1)
                wait_past(dve, f"stored{half}", 16 * earlier)
                nc.vector.tensor_tensor(by_step(o_sb[:, half, :]), by_step(mix_bank[:, :]), h2_rows(g), ALU.add)\
                    .then_inc(S["out_ready"], 1)

            def split_z(g, n, half):
                dve.wait_ge(S["zhi_ready"], n + 1)
                wait_past(dve, "fc1_done", E * (n - 1))
                nc.vector.tensor_tensor(part_lo[:, half, :], z2_cols(g), part_hi[:, half, :].bitcast(F32), ALU.subtract)\
                    .then_inc(S["zlo_ready"], 1)

            def group(g, n, half, pair, more=True, before=True, a=None, b=None):
                if more:
                    gates_a(n + 1)
                if before:
                    weigh(n - 1)
                unit(n, 1, half)
                if a:
                    a()
                if more:
                    split_z(g + 1, n + 1, 1 - half)
                    gates_b(n + 1)
                if b:
                    b()
                if before:
                    add_up(g - 1, n - 1, 1 - half, pair - (1 - half))

            def experts(n0, hooks):
                m0 = n0 // 2
                for g in range(4):
                    group(g, n0 + g, g % 2, m0 + g // 2, before=(g > 0), **hooks.get(g, {}))
                with dve.Fori(2, GROUPS // 2 - 1) as p:
                    for half in range(2):
                        group(2 * p + half, n0 + 2 * p + half, half, m0 + p)
                for half in range(2):
                    g = GROUPS - 2 + half
                    group(g, n0 + g, half, m0 + g // 2, more=(half == 0))
                n = n0 + GROUPS - 1
                dve.wait_ge(S["wf_ready"], n + 1)
                dve.wait_ge(S["mix_done"], n)
                for (cols, low_b, mix_b), ready, signal in zip(
                        tail, (("first_low", n0 // GROUPS + 1), ("low_done", n + 1)),
                        ("first_weighed", "low_ready")):
                    dve.wait_ge(S[ready[0]], ready[1])
                    nc.vector.tensor_tensor(low[:, cols], low_b[:, cols], w_feat[:, cols], ALU.mult)\
                        .then_inc(S[signal], 1)
                dve.wait_ge(S["stored1"], 16 * (n // 2))
                for i, ((cols, low_b, mix_b), ready, signal) in enumerate(zip(
                        tail, (("first_mixed", n0 // GROUPS + 1), ("mix_done", n + 1)),
                        ("first_out", "out_ready"))):
                    dve.wait_ge(S[ready[0]], ready[1])
                    nc.vector.tensor_tensor(
                        o_sb[:, 1, cols].rearrange("p (j c) -> p j c", c=P),
                        mix_b[:, cols].rearrange("p (j c) -> p j c", c=P),
                        state[:, 0, G * (GROUPS - 1) + 1 + i * G // 2:G * (GROUPS - 1) + 1 + (i + 1) * G // 2, :],
                        ALU.add).then_inc(S[signal], 1)

            for g in range(2):
                main(g, g)
            with dve.Fori(1, GROUPS // 2 - 1) as p:
                for parity in range(2):
                    main(2 * p + parity, parity)
            for g in (GROUPS - 2, GROUPS - 1):
                main(g, g % 2)

            dve.wait_ge(S["state0"], WARM + STEPS + 1)
            dve.wait_ge(S["state1"], WARM + STEPS + 1)
            nc.vector.tensor_tensor(diff[:, :, 0:COLS], state[:, :, 0, B:P], state[:, :, STEPS, 0:COLS],
                                    ALU.subtract).then_inc(S["diff_done"], 1)
            gates_b(0)
            dve.wait_ge(S["diff_turned"], 1)
            turned = cmp_bank[0:COLS, :].rearrange("p (a c) -> p a c", a=2)
            nc.vector.tensor_reduce(cmp_col[0:COLS, 0:2], turned, AX_X, ALU.max)
            nc.vector.tensor_reduce(cmp_col[0:COLS, 2:3], turned[:, 0, :], AX_X, ALU.min)\
                .then_inc(S["cmp_step"], 1)

            def agreement():
                dve.wait_ge(S["cmp_step"], 1)
                nc.vector.scalar_tensor_tensor(cmp_col[0:COLS, 3:4], cmp_col[0:COLS, 2:3], -1.0,
                                               cmp_col[0:COLS, 0:1], ALU.mult, ALU.max).then_inc(S["cmp_step"], 1)
                dve.wait_ge(S["cmp_step"], 2)
                nc.vector.scalar_tensor_tensor(agree[0:COLS, :], cmp_col[0:COLS, 1:2], TOL,
                                               cmp_col[0:COLS, 3:4], ALU.mult, ALU.is_ge).then_inc(S["cmp_step"], 1)

            def verdict():
                dve.wait_ge(S["cmp_turned"], 1)
                nc.vector.tensor_reduce(ok_f[:, :], cmp_bank[0:1, 0:COLS], AX_X, ALU.min)\
                    .then_inc(S["cmp_step"], 1)
                dve.wait_ge(S["cmp_step"], 4)
                nc.vector.tensor_copy(ok_i[:, :], ok_f[:, :]).then_inc(S["ok_ready"], 1)

            def last_stats():
                h2_stats(GROUPS - 1, GROUPS - 1)
                h2_moments(GROUPS - 1)

            experts(0, {0: {"a": agreement, "b": verdict},
                        1: {"a": lambda: h2_stats(GROUPS - 2, GROUPS - 2),
                            "b": lambda: (h2_moments(GROUPS - 2), h2(GROUPS - 1, GROUPS - 1))},
                        2: {"a": lambda: h2_norm(GROUPS - 2, GROUPS - 2), "b": last_stats},
                        3: {"a": lambda: h2_norm(GROUPS - 1, GROUPS - 1)}})
            dve.wait_ge(S["ok_ready"], 1)
            ok = dve.value_load(ok_i[0:1, 0:1], min_val=0, max_val=1)
            with dve.If(ok == 0):
                def redo_step(n, s, col):
                    dve.wait_ge(S["redo_pre"], n + 1)
                    for m in range(KH):
                        last = nc.vector.tensor_scalar(
                            state[:, m, bass.ds(s + 1, 1), bass.ds(col, B)], bank[m][:, 0:B],
                            bias_h[:, m:m + 1], 0.0, ALU.add, ALU.max)
                    last.then_inc(S["redo_state"], 1)

                dve.wait_ge(S["out_ready"], GROUPS)
                nc.vector.memset(state[:, :, 0, 0:B], 0.0).then_inc(S["redo_state"], 1)
                with dve.Fori(0, CHUNKS - 1) as c:
                    with dve.Fori(0, STEPS) as s:
                        redo_step(c * STEPS + s, s, c * B)
                    dve.wait_ge(S["redo_state"], (c + 1) * (STEPS + 1))
                    nc.vector.tensor_copy(state[:, :, 0, bass.ds(c * B + B, B)],
                                          state[:, :, STEPS, bass.ds(c * B, B)]).then_inc(S["redo_state"], 1)
                with dve.Fori(0, STEPS) as s:
                    redo_step((CHUNKS - 1) * STEPS + s, s, COLS)
                with dve.Fori(0, GROUPS) as q:
                    h2(q, GROUPS + q)
                    h2_stats(q, GROUPS + q)
                    h2_moments(GROUPS + q)
                    h2_norm(q, GROUPS + q)
                split_z(0, GROUPS, 0)
                gates_a(GROUPS)
                gates_b(GROUPS)
                experts(GROUPS, {})
            dve.end_ifs()

        @block.tensor
        def _(pe):
            def turn(n):
                b, sources, loads = prep[n - 1]
                for name, count in loads:
                    pe.wait_ge(S[name], 16 * count)
                for i, (src, rows, cols) in enumerate(sources):
                    last = nc.tensor.transpose(bank[b][0:cols, i * P:i * P + rows], src, ident[0:rows, 0:rows])
                last.then_inc(S["prep_done"], 1)

            def keep_clock(place, n):
                for _ in range(n):
                    nc.tensor.transpose(place[:, 0:P], ident[:, :], ident[:, :])

            pe.wait_ge(S["ident_made"], 1)
            keep_clock(bank[7], 12)
            turn(PREP_TOK)

            def patches(g, half):
                if isinstance(g, int) and g < 2:
                    pe.wait_ge(S["x_landed"], 32)
                    frames = x_sb[:, g * G * D:g * G * D + XW]
                else:
                    pe.wait_ge(S["piece_ready"], g - 1)
                    frames = x_piece[:, half, :]
                wait_past(pe, "patch_copied", g - 1)
                for j in range(G):
                    last = nc.tensor.transpose(bank[4 + half][0:PATCH, one(j)],
                                               frames[:, j * D:j * D + PATCH], ident[:, :])
                last.then_inc(S["patch_done"], 1)

            def tdnn(g, half):
                pe.wait_ge(S["patch_copied"], g + 1)
                wait_past(pe, "y_ready", g - 1)
                nc.tensor.matmul(bank[6 + half][:, :], tokw_t[:, :], patch_t[:, half, :], start=True, stop=True)\
                    .then_inc(S["y_done"], 1)

            patches(0, 0)
            patches(1, 1)
            pe.wait_ge(S["prep_copied"], PREP_TOK)
            tdnn(0, 0)
            patches(2, 0)
            tdnn(1, 1)
            patches(3, 1)
            tdnn(2, 0)
            with pe.Fori(2, GROUPS // 2) as p:
                patches(2 * p, 0)
                tdnn(2 * p - 1, 1)
                patches(2 * p + 1, 1)
                tdnn(2 * p, 0)
            tdnn(GROUPS - 1, 1)
            turn(PREP_IH)
            turn(PREP_FC1)
            turn(PREP_HH)
            turn(PREP_OUT)
            pe.wait_ge(S["y_ready"], GROUPS)
            turn(PREP_FC2)

            def ln1_turn(u, half, j0=0):
                pe.wait_ge(S["hb_ready"], u + 1)
                wait_past(pe, "h_kept", u - 1)
                for j in range(j0, G):
                    last = nc.tensor.transpose(h_bank[half][:, one(j)], hb[:, half, one(j)], ident[:, :])
                last.then_inc(S["h_done"], 1)

            def ln1_back(u, half, j0=0):
                pe.wait_ge(S["z_ready"], u + 1)
                wait_past(pe, "a_ready", u - 1)
                for j in range(j0, G):
                    last = nc.tensor.transpose(z_bank[half][:, one(j)], z_sb[:, half, one(j)], ident[:, :])
                last.then_inc(S["z_done"], 1)

            pe.wait_ge(S["patch_copied"], GROUPS)
            keep_clock(bank[4], 9)
            pe.wait_ge(S["prep_copied"], PREP_FC2)
            for e in range(E):
                last = nc.tensor.matmul(h_bank[1][ER * e:ER * (e + 1), 0:P], lorab_t[:, e, :],
                                        fc2_t[:, one(e)], start=True, stop=True)
            last.then_inc(S["prep_done"], 1)
            keep_clock(bank[4], 3)
            pe.wait_ge(S["head_step"], HEAD_HB)
            nc.tensor.transpose(head_bank[:, 0:P], hb[:, 0, 0:P], ident[:, :]).then_inc(S["head_step"], 1)
            ln1_turn(0, 0, j0=1)
            pe.wait_ge(S["adapt_done"], 1)
            ln1_turn(1, 1)
            keep_clock(z_bank[0], 7)
            pe.wait_ge(S["head_step"], HEAD_Z)
            nc.tensor.transpose(z_bank[0][:, 0:P], z_sb[:, 0, 0:P], ident[:, :]).then_inc(S["head_step"], 1)

            def project(parity, j0, j1, at):
                for m in range(KH):
                    nc.tensor.matmul(rb[m][parity][:, j0 * P:j1 * P], wih_t[:, one(m)],
                                     a_in[:, at * W + j0 * P:at * W + j1 * P], start=True, stop=True)

            def project_whole(parity, m, at):
                nc.tensor.matmul(rb[m][parity][:, :], wih_t[:, one(m)], a_in[:, bass.ds(at * W, W)],
                                 start=True, stop=True)

            def project_parts(g, parity, m):
                n = split_of(g)
                if m == 0:
                    pe.wait_ge(S["in_hi_ready"], n + 1)
                    pe.wait_ge(S["in_lo_ready"], n + 1)
                for i, (w, a) in enumerate(((wih_hi, part_hi), (wih_hi, part_lo), (wih_lo, part_hi))):
                    mm = nc.tensor.matmul(rb[m][parity][:, :], w[:, one(m)], a[:, parity, :],
                                          start=(i == 0), stop=(i == 2))
                if m == KH - 1:
                    mm.then_inc(S["in_used"], 1)

            def recur(n, parity, j, rhs, cols, last):
                for m in range(KH):
                    for k in range(KH):
                        if m == 0:
                            pe.wait_ge(S["state0" if k == 0 else "state1"], n + 1)
                        mm = nc.tensor.matmul(rb[m][parity][:, j * P:j * P + cols], whh_t[:, one(m * KH + k)],
                                              rhs(k), start=False, stop=(k == KH - 1),
                                              skip_group_check=True)
                    mm.then_inc(S["pre0" if m == 0 else "pre1"], 1)

            pe.wait_ge(S["fc1_split"], 1)
            pe.wait_ge(S["head_step"], HEAD_A)
            project(HEAD_PARITY, 0, 1, FIRST)

            for i in range(WARMUPS):
                a, b = 2 * i + 2, 2 * i + 3
                parity = (i - WARMUPS) % 2
                for j in range(G):
                    recur(G * i + j, HEAD_PARITY if i == j == 0 else parity, j,
                          lambda k: state[:, k, j % 2, B:P], COLS, j == G - 1 or i == j == 0)
                    if i == 0 and j == 0:
                        ln1_back(0, 0, j0=1)
                        ln1_turn(2, 0)
                        pe.wait_ge(S["a_ready"], 1)
                        pe.wait_ge(S["head_kept"], 1)
                        project(parity, 1, G, FIRST)
                    elif i + 1 < WHOLE:
                        if j == 3 or (i > 0 and j == 2):
                            pe.wait_ge(S["a_ready"], i + 2)
                            for m in (range(KH) if i == 0 else (j - 2,)):
                                project_whole(1 - parity, m, FIRST + i + 1)
                    elif j >= 2:
                        if i + 1 == WHOLE and j == 2:
                            pe.wait_ge(S["rnn_split"], 2)
                        project_parts(i + 1 - WARMUPS, 1 - parity, j - 2)
                    if j == 0:
                        ln1_back(b - 2, 1)
                    elif j == 1:
                        ln1_turn(b, 1)
                    elif j == 2 and i < WARMUPS - 1:
                        ln1_turn(a + 2, 0)
                    elif j == 3 and i < WARMUPS - 1:
                        ln1_back(a, 0)

            def w_out(q, k, n):
                if k == 0:
                    wait_past(pe, "hf_ready", n)
                mm = nc.tensor.matmul(wo_bank[:, :], wout_t[:, one(k)], state[:, k, bass.ds(G * q + 1, G), :],
                                      start=(k == 0), stop=(k == KH - 1))
                if k == KH - 1:
                    mm.then_inc(S["wout_done"], 1)

            def w_out_parts(n, k):
                if k == 0:
                    wait_past(pe, "hf_ready", n)
                pe.wait_ge(S[f"state_hi_ready{k}"], n + 1)
                pe.wait_ge(S[f"state_lo_ready{k}"], n + 1)
                for i, (w, h) in enumerate(((wout_hi, state_hi), (wout_hi, state_lo), (wout_lo, state_hi))):
                    mm = nc.tensor.matmul(wo_bank[:, :], w[:, one(k)], h[:, k, :],
                                          start=(k == 0 and i == 0), stop=(k == KH - 1 and i == 2))
                if k == KH - 1:
                    mm.then_inc(S["wout_done"], 1)

            def h2_turn(n):
                pe.wait_ge(S["hf_ready"], n + 1)
                wait_past(pe, "h2_ready", n)
                for j in range(G):
                    last = nc.tensor.transpose(h2_bank[:, one(j)], h_feat[:, one(j)], ident[:, :])
                last.then_inc(S["h2_done"], 1)

            def z2_turn(n):
                pe.wait_ge(S["z2_ready"], n + 1)
                wait_past(pe, "zf_ready", n)
                for j in range(G):
                    last = nc.tensor.transpose(z2_bank[:, one(j)], z_sb[:, 0, one(j)], ident[:, :])
                last.then_inc(S["z2_done"], 1)

            def main(g, parity):
                first = isinstance(g, int)
                more = not first or g < GROUPS - 1
                for j in range(G):
                    recur(WARM + G * g + j, parity, j, lambda k: state[:, k, bass.ds(G * g + j, 1), :], P,
                          j == G - 1)
                    if first and g == 0:
                        if j == 0:
                            ln1_back(GROUPS - 2, 0)
                        elif j == 2:
                            ln1_back(GROUPS - 1, 1)
                        else:
                            project_parts(1, 1, j // 2)
                    elif j == 0 and more:
                        for m in range(KH):
                            project_parts(g + 1, 1 - parity, m)
                    if first and g == 1 and j == 0:
                        pe.wait_ge(S["a_ready"], GROUPS)
                    if not first or g >= 1:
                        if j in (1, 2):
                            w_out_parts(g - 1, j - 1)
                        elif j == 3:
                            h2_turn(g - 1)
                    if j == 3 and (not first or g >= 2):
                        z2_turn(g - 2)
                    if not more:
                        if j == 0:
                            gate(0, 0)
                        elif j == 1:
                            gate_turn(0)
                        elif j == 3:
                            gate(1, 1)

            def gate(n, half):
                pe.wait_ge(S["zc_ready"], n + 1)
                wait_past(pe, "gate_step", 10 * n - 7)
                for j in range(G):
                    last = nc.tensor.matmul(gate_bank[ER * j:ER * (j + 1), 0:P], gate_t[:, :],
                                            z_feat[:, half, one(j)], start=True, stop=True)
                last.then_inc(S["gate_done"], 1)

            def gate_turn(n):
                pe.wait_ge(S["logit_ready"], n + 1)
                nc.tensor.transpose(gate_bank[:, P:2 * P], logit_f[:, :], ident[:, :]).then_inc(S["logit_turned"], 1)

            def fc1(n, e, half):
                if e == 3:
                    pe.wait_ge(S["hidden_dve"], n + 1)
                else:
                    wait_past(pe, "hidden_act", 3 * n + (-1, 0, 1)[e])
                if e == 0:
                    pe.wait_ge(S["zhi_ready"], n + 1)
                    pe.wait_ge(S["zlo_ready"], n + 1)
                for i, (w, z) in enumerate(((fc1_hi, part_hi), (fc1_hi, part_lo), (fc1_lo, part_hi))):
                    mm = nc.tensor.matmul(fc_bank[e % 2][:, :], w[:, one(e)], z[:, half, :],
                                          start=(i == 0), stop=(i == 2))
                mm.then_inc(S["fc1_done"], 1)

            def low_rank(n, half):
                pe.wait_ge(S["hidden_act"], 3 * n + 3)
                pe.wait_ge(S["hidden_dve"], n + 1)
                wait_past(pe, "low_ready", n)
                for e in range(E):
                    last = nc.tensor.matmul(low_bank[ER * e:ER * (e + 1), :], lora_a_sb[:, e, :],
                                            hidden[:, half, e, :], start=True, stop=True)
                last.then_inc(S["low_done"], 1)

            def w_turn(n):
                pe.wait_ge(S["w_ready"], n + 1)
                wait_past(pe, "wf_ready", n)
                for j in range(G):
                    last = nc.tensor.transpose(w_bank[:, one(j)], w_wide[:, j, :, :], ident[:, :])
                last.then_inc(S["w_turned"], 1)

            def mix(n):
                pe.wait_ge(S["low_ready"], n + 1)
                wait_past(pe, "out_ready", n)
                for j in range(G):
                    last = nc.tensor.matmul(mix_bank[:, one(j)], low[:, one(j)], adapt[:, :], start=True, stop=True)
                last.then_inc(S["mix_done"], 1)

            def group(n, half, left=2, before=True, a=None, b=None, c=None, d=None):
                fc1(n, 0, half)
                if left >= 1:
                    gate_turn(n + 1)
                if before:
                    low_rank(n - 1, 1 - half)
                if a:
                    a()
                fc1(n, 1, half)
                if b:
                    b()
                fc1(n, 2, half)
                w_turn(n)
                if before:
                    mix(n - 1)
                if c:
                    c()
                fc1(n, 3, half)
                if left >= 2:
                    gate(n + 2, half)
                if d:
                    d()

            def experts(n0, hooks):
                for g in range(4):
                    group(n0 + g, g % 2, before=(g > 0), **hooks.get(g, {}))
                with pe.Fori(2, GROUPS // 2 - 1) as p:
                    for half in range(2):
                        group(n0 + 2 * p + half, half)
                group(n0 + GROUPS - 2, 0, left=1)
                group(n0 + GROUPS - 1, 1, left=0)
                n = n0 + GROUPS - 1
                pe.wait_ge(S["hidden_act"], 3 * n + 3)
                pe.wait_ge(S["hidden_dve"], n + 1)
                pe.wait_ge(S["low_ready"], n)
                for (cols, low_b, mix_b), signal in zip(tail, ("first_low", "low_done")):
                    for e in range(E):
                        last = nc.tensor.matmul(low_b[ER * e:ER * (e + 1), cols], lora_a_sb[:, e, :],
                                                hidden[:, 1, e, cols], start=True, stop=True)
                    last.then_inc(S[signal], 1)
                pe.wait_ge(S["out_ready"], n)
                for i, ((cols, low_b, mix_b), ready, signal) in enumerate(zip(
                        tail, (("first_weighed", n0 // GROUPS + 1), ("low_ready", n + 1)),
                        ("first_mixed", "mix_done"))):
                    pe.wait_ge(S[ready[0]], ready[1])
                    for j in range(i * G // 2, (i + 1) * G // 2):
                        last = nc.tensor.matmul(mix_b[:, one(j)], low[:, one(j)], adapt[:, :],
                                                start=True, stop=True)
                    last.then_inc(S[signal], 1)

            def compare():
                pe.wait_ge(S["diff_done"], 1)
                for k in range(KH):
                    nc.tensor.transpose(cmp_bank[0:COLS, one(k)], diff[:, k, 0:COLS], ident[:, :])
                    last = nc.tensor.transpose(cmp_bank[0:COLS, one(KH + k)], state[:, k, STEPS, 0:COLS],
                                               ident[:, :])
                last.then_inc(S["diff_turned"], 1)

            def finish_rnn():
                for k in range(KH):
                    w_out_parts(GROUPS - 1, k)

            def turn_agreement():
                pe.wait_ge(S["cmp_step"], 3)
                nc.tensor.transpose(cmp_bank[0:1, 0:COLS], agree[0:COLS, :], ident[0:COLS, 0:COLS])\
                    .then_inc(S["cmp_turned"], 1)

            def last_turn():
                pe.wait_ge(S["cmp_step"], 4)
                h2_turn(GROUPS - 1)

            pe.wait_ge(S["h_kept"], GROUPS)
            for g in range(2):
                main(g, g)
            with pe.Fori(1, GROUPS // 2 - 1) as p:
                for parity in range(2):
                    main(2 * p + parity, parity)
            for g in (GROUPS - 2, GROUPS - 1):
                main(g, g % 2)
            pe.wait_ge(S["state0"], WARM + STEPS + 1)
            pe.wait_ge(S["state1"], WARM + STEPS + 1)
            experts(0, {0: {"a": compare, "b": finish_rnn, "c": turn_agreement},
                        1: {"c": last_turn},
                        2: {"d": lambda: z2_turn(GROUPS - 2)},
                        3: {"d": lambda: z2_turn(GROUPS - 1)}})
            pe.wait_ge(S["ok_ready"], 1)
            ok = pe.value_load(ok_i[0:1, 0:1], min_val=0, max_val=1)
            with pe.If(ok == 0):
                def redo_step(n, s, col):
                    pe.wait_ge(S["redo_state"], n)
                    for m in range(KH):
                        nc.tensor.matmul(bank[m][:, 0:B], wih_t[:, one(m)],
                                         a_in[:, bass.ds(s * P + col, B)], start=True, stop=False)
                        for k in range(KH):
                            last = nc.tensor.matmul(
                                bank[m][:, 0:B], whh_t[:, one(m * KH + k)],
                                state[:, k, bass.ds(s, 1), bass.ds(col, B)], start=False, stop=(k == KH - 1))
                    last.then_inc(S["redo_pre"], 1)

                with pe.Fori(0, CHUNKS - 1) as c:
                    with pe.Fori(0, STEPS) as s:
                        redo_step(c * (STEPS + 1) + s + 1, s, c * B)
                with pe.Fori(0, STEPS) as s:
                    redo_step((CHUNKS - 1) * (STEPS + 1) + s + 1, s, COLS)
                pe.wait_ge(S["redo_state"], CHUNKS * (STEPS + 1))
                pe.wait_ge(S["out_ready"], GROUPS)
                with pe.Fori(0, GROUPS) as q:
                    for k in range(KH):
                        w_out(q, k, GROUPS + q)
                    h2_turn(GROUPS + q)
                    z2_turn(GROUPS + q)
                gate(GROUPS, 0)
                gate_turn(GROUPS)
                gate(GROUPS + 1, 1)
                experts(GROUPS, {})
            pe.end_ifs()


_INS = ['x', 'L0_tok_W', 'L0_tok_b', 'L0_tok_gamma', 'L0_tok_beta', 'L0_attn_W_ih', 'L0_attn_W_hh',
        'L0_attn_b_ih', 'L0_attn_b_hh', 'L0_attn_W_out', 'L0_attn_b_out', 'L0_ffn_gate_w', 'L0_ffn_thr_w',
        'L0_ffn_fc1_w', 'L0_ffn_lora_A', 'L0_ffn_lora_B', 'L0_ffn_fc2_w']


def kernel(**inputs):
    import numpy as _np
    import concourse.bacc as _bacc
    from concourse import mybir as _mybir
    from concourse.bass_utils import run_bass_kernel_spmd as _run

    nc = _bacc.Bacc("TRN2", target_bir_lowering=False, num_devices=1)
    arrays, args = {}, []
    for name in _INS:
        a = _np.ascontiguousarray(inputs[name])
        arrays[f"in_{name}_dram"] = a
        args.append(nc.dram_tensor(f"in_{name}_dram", a.shape, _mybir.dt.from_np(a.dtype), kind="ExternalInput").ap())
    B, T, D = inputs['x'].shape
    O, F = inputs['L0_tok_W'].shape
    out = nc.dram_tensor("out_dram", (B, T - F // D + 1, O), _mybir.dt.float32, kind="ExternalOutput").ap()
    audio_tower(nc, *args, out)
    r = _run(nc, [arrays], core_ids=[0])
    return r.results[0]["out_dram"]
```
